# Optimizing a Trainium2 kernel written in Bass

```python
import numpy as np
import jax
import jax.numpy as jnp

def _softmax(x, axis=-1):
    return jax.nn.softmax(x, axis=axis)

def _gelu(x):
    return jax.nn.gelu(x, approximate=True)

def _silu(x):
    return jax.nn.silu(x)

def _sigmoid(x):
    return jax.nn.sigmoid(x)

def _layernorm(x, axis=-1, eps=1e-05):
    m = jnp.mean(x, axis=axis, keepdims=True)
    v = jnp.var(x, axis=axis, keepdims=True)
    return (x - m) / jnp.sqrt(v + eps)

def _scatter_add(tgt, idx, src, axis=0):
    return tgt.at[idx].add(src)

def _segment_sum(src, seg, n):
    return jax.ops.segment_sum(src, seg, n)
kernel_name = 'mk_gnn_resnorm_d2_gnn_r8_1fa59f'

def setup_inputs(seed: int=0):
    np.random.seed(seed)
    _w = jnp.asarray

    def _rec_inputs():
        import jax
        import jax.numpy as jnp
        _gk = jax.random.key(seed)
        x = -0.000202 + 1 * jax.random.normal(jax.random.fold_in(_gk, 1), (6250, 128), jnp.float32)
        src = jax.random.randint(jax.random.fold_in(_gk, 2), (100000,), 0, 6250, jnp.int32)
        dst = jax.random.randint(jax.random.fold_in(_gk, 3), (100000,), 0, 6250, jnp.int32)
        _o = jnp.argsort(dst, stable=True)
        src = src[_o]
        dst = dst[_o]
        edge_attr_128 = -8.16379e-05 + 0.999858 * jax.random.normal(jax.random.fold_in(_gk, 12), (100000, 128), jnp.float32)
        edge_weight = jax.random.uniform(jax.random.fold_in(_gk, 14), (100000,), jnp.float32, 0.0, 0.999998)
        return (x, src, dst, edge_attr_128, edge_weight)
    x, src, dst, edge_attr_128, edge_weight = _rec_inputs()

    def _L0_gnn_setup():
        import jax, jax.numpy as jnp
        import numpy as np
        N = 6250
        E = 75000
        D_IN = 128
        D_HID = 128

        def gcn_conv(x, src, dst, ew, W, b):
            n = x.shape[0]
            deg = jax.ops.segment_sum(ew, dst, num_segments=n)
            dinv = jnp.where(deg > 0, jax.lax.rsqrt(deg), 0.0)
            norm = dinv[src] * ew * dinv[dst]
            h = x @ W
            msg = h[src] * norm[:, None]
            out = jax.ops.segment_sum(msg, dst, num_segments=n)
            return out + b
        key = jax.random.key(seed)
        k1, k2, k3, k4, k5, k6, k7 = jax.random.split(key, 7)
        x = jax.random.normal(k1, (N, D_IN), dtype=jnp.float32)
        edge_index = jax.random.randint(k2, (2, E), 0, N, dtype=jnp.int64)
        edge_weight = jax.random.uniform(k3, (E,), dtype=jnp.float32)
        s1 = 1.0 / np.sqrt(D_IN)
        s2 = 1.0 / np.sqrt(D_HID)
        W1 = jax.random.uniform(k4, (D_IN, D_HID), dtype=jnp.float32, minval=-s1, maxval=s1)
        b1 = jax.random.uniform(k5, (D_HID,), dtype=jnp.float32, minval=-s1, maxval=s1)
        W2 = jax.random.uniform(k6, (D_HID, D_IN), dtype=jnp.float32, minval=-s2, maxval=s2)
        b2 = jax.random.uniform(k7, (D_IN,), dtype=jnp.float32, minval=-s2, maxval=s2)
        return {'x': x, 'edge_index': edge_index, 'edge_weight': edge_weight, 'W1': W1, 'b1': b1, 'W2': W2, 'b2': b2}
    _L0_gnn_all = _L0_gnn_setup()
    _L0_gnn_in = {k: v for k, v in _L0_gnn_all.items() if k in ('W1', 'b1', 'W2', 'b2')}
    del _L0_gnn_all

    def _L1_gnn_setup():
        import jax, jax.numpy as jnp
        import numpy as np
        NEG_SLOPE = 0.01
        key = jax.random.key(seed)
        ks = jax.random.split(key, 8)
        N, E, D = (6250, 100000, 128)
        return {'h': jax.random.normal(ks[0], (N, D), jnp.float32), 'r_h': jax.random.normal(ks[1], (E, D), jnp.float32), 'fc_w': jax.random.normal(ks[2], (D, D), jnp.float32) * 0.05, 'fc_r_w': jax.random.normal(ks[3], (D, D), jnp.float32) * 0.05, 'attn_w': jax.random.normal(ks[4], (1, 3 * D), jnp.float32) * 0.05, 'loop_w': jax.random.normal(ks[5], (D, D), jnp.float32) * 0.05, 'src': jax.random.randint(ks[6], (E,), 0, N, jnp.int32), 'dst': jax.random.randint(ks[7], (E,), 0, N, jnp.int32)}
    _L1_gnn_all = _L1_gnn_setup()
    _L1_gnn_in = {k: v for k, v in _L1_gnn_all.items() if k in ('fc_w', 'fc_r_w', 'attn_w', 'loop_w')}
    del _L1_gnn_all
    return {'x': x, 'src': src, 'dst': dst, 'edge_attr_128': edge_attr_128, 'edge_weight': edge_weight, 'L0_gnn_W1': _L0_gnn_in['W1'], 'L0_gnn_b1': _L0_gnn_in['b1'], 'L0_gnn_W2': _L0_gnn_in['W2'], 'L0_gnn_b2': _L0_gnn_in['b2'], 'L1_gnn_fc_w': _L1_gnn_in['fc_w'], 'L1_gnn_fc_r_w': _L1_gnn_in['fc_r_w'], 'L1_gnn_attn_w': _L1_gnn_in['attn_w'], 'L1_gnn_loop_w': _L1_gnn_in['loop_w']}

def reference(x, src, dst, edge_attr_128, edge_weight, L0_gnn_W1, L0_gnn_b1, L0_gnn_W2, L0_gnn_b2, L1_gnn_fc_w, L1_gnn_fc_r_w, L1_gnn_attn_w, L1_gnn_loop_w):
    import jax
    import jax.numpy as jnp

    def _L0_gnn_ref(x, edge_index, edge_weight, W1, b1, W2, b2):
        import jax, jax.numpy as jnp
        import numpy as np
        N = 6250
        E = 75000
        D_IN = 128
        D_HID = 128

        def gcn_conv(x, src, dst, ew, W, b):
            n = x.shape[0]
            deg = jax.ops.segment_sum(ew, dst, num_segments=n)
            dinv = jnp.where(deg > 0, jax.lax.rsqrt(deg), 0.0)
            norm = dinv[src] * ew * dinv[dst]
            h = x @ W
            msg = h[src] * norm[:, None]
            out = jax.ops.segment_sum(msg, dst, num_segments=n)
            return out + b
        n = x.shape[0]
        loops = jnp.arange(n, dtype=edge_index.dtype)
        src = jnp.concatenate([edge_index[0], loops])
        dst = jnp.concatenate([edge_index[1], loops])
        ew = jnp.concatenate([edge_weight, jnp.ones((n,), dtype=edge_weight.dtype)])
        h = gcn_conv(x, src, dst, ew, W1, b1)
        h = jax.nn.relu(h)
        h = gcn_conv(h, src, dst, ew, W2, b2)
        return jax.nn.sigmoid(h)

    def _L1_gnn_ref(h, r_h, fc_w, fc_r_w, attn_w, loop_w, src, dst):
        import jax, jax.numpy as jnp
        import numpy as np
        NEG_SLOPE = 0.01
        N, D = h.shape
        z = h @ fc_w.T
        rh = r_h @ fc_r_w.T
        zs = z[src]
        zd = z[dst]
        aw = attn_w.reshape(3, D)
        e = zs @ aw[0] + zd @ aw[1] + rh @ aw[2]
        e = jnp.where(e >= 0, e, NEG_SLOPE * e)
        m = jax.ops.segment_max(e, dst, num_segments=N)
        ex = jnp.exp(e - m[dst])
        den = jax.ops.segment_sum(ex, dst, num_segments=N)
        alpha = ex / den[dst]
        msg = alpha[:, None] * (zs + rh)
        agg = jax.ops.segment_sum(msg, dst, num_segments=N)
        out = jax.nn.relu(agg + z @ loop_w)
        return out
    edge_index = jnp.stack([src, dst])
    x = _layernorm(x + _L0_gnn_ref(x, edge_index, edge_weight, L0_gnn_W1, L0_gnn_b1, L0_gnn_W2, L0_gnn_b2), axis=-1)
    x = _layernorm(x + _L1_gnn_ref(x, edge_attr_128, L1_gnn_fc_w, L1_gnn_fc_r_w, L1_gnn_attn_w, L1_gnn_loop_w, src, dst), axis=-1)
    return x

_drawn_inputs = setup_inputs


def setup_inputs(seed=0):
    import zlib

    import numpy as np

    out = dict(_drawn_inputs(seed))
    spreads = {}
    factors = {'edge_weight': 8.0,
     'L0_gnn_W1': 8.0,
     'L0_gnn_b1': 8.0,
     'L0_gnn_W2': 4.435,
     'L0_gnn_b2': 3.865}
    for name, (base, spread) in spreads.items():
        noise = np.random.default_rng([zlib.crc32(name.encode()), seed]).standard_normal(out[name].shape)
        drawn = base * np.exp(spread * noise) if base else spread * noise
        out[name] = jnp.asarray(drawn.astype(out[name].dtype))
    for name, factor in factors.items():
        out[name] = (out[name] * factor).astype(out[name].dtype)
    return out
```

```python
import concourse.bass as bass
from concourse import mybir
from contextlib import ExitStack

FP32 = mybir.dt.float32
BF16 = mybir.dt.bfloat16
I32 = mybir.dt.int32
ALU = mybir.AluOpType
ACT = mybir.ActivationFunctionType
AX = mybir.AxisListType

N, E, D = 6250, 100000, 128
P = 128
W = 128
GT = 8
GE = GT * P
G = -(-E // GE)
T = G * GT
EB = -(-T // P)
TP = EB * P
RG = 14
IT = G // RG
RT = RG * GT
NB = -(-N // P)
NC = 7
NCH = NB // NC
NLAST = N - (NB - 1) * P
NA = NB * P + W
FT = E // P
FR = E - FT * P
LP, LW = 125, 800
FAR = float(1 << 20)
BIG = 1.0e30
EPS = 1.0e-5
SLOPE = 0.01
assert G * GE == T * P and IT * RG == G and NCH * NC == NB and LP * LW == E


def build(nc, x, src, dst, edge_attr, edge_weight, W1, b1, W2, b2, fc_w, fc_r_w, attn_w, loop_w, out):
    ctx = ExitStack()
    with ctx:
        def sb(name, shape, dt=FP32):
            return ctx.enter_context(nc.sbuf_tensor(name, shape, dt))

        def sem(name):
            return ctx.enter_context(nc.semaphore(name))

        def scratch(name, shape, dt=FP32):
            return nc.dram_tensor(name, shape, dt).ap()

        x1_d = scratch("x1_d", (NB * P, D))
        h1_d = scratch("h1_d", (NB * P, D))
        x2_d = scratch("x2_d", (NB * P, D))
        lo_d = scratch("lo_d", (TP * P,), BF16)
        rank_d = scratch("rank_d", (TP * P,), BF16)
        basef_d = scratch("basef_d", (EB * 16,))
        basei_d = scratch("basei_d", (EB * 16,), I32)
        s1_d = scratch("s1_d", (3, NB * P), BF16)
        e_d = scratch("e_d", (TP * P,))
        al_d = scratch("al_d", (E,))

        iota_i = sb("iota_i", [P, P], I32)
        pidx_i = sb("pidx_i", [P, 1], I32)
        iota = sb("iota", [P, P])
        iota_h = sb("iota_h", [P, P], BF16)
        pidx = sb("pidx", [P, 1])
        ident = sb("ident", [P, P])
        ident_h = sb("ident_h", [P, P], BF16)
        ones_h = sb("ones_h", [P, 1], BF16)
        ones3 = sb("ones3", [3, 1])
        acc = sb("acc", [P, 2, NA])
        rows = acc[:, 1, 0:NB * D].rearrange("p (b d) -> p b d", d=D)
        erow = acc[:, 1, 0:7 * TP].rearrange("p (a b t) -> p a b t", a=7, t=P)
        srcR, dstR, loI = (erow[:, k].bitcast(I32) for k in range(3))
        ewR, rowF = erow[:, 3], erow[:, 4:7]
        s1P = acc[:, 1, 0:NA // 2].bitcast(BF16)
        loH = sb("loH", [P, EB, P], BF16)
        lin = acc[0:LP, 0, 0:6 * LW].rearrange("p (k j) -> p k j", k=6)
        dL, dprevL, dnextL = (lin[:, k].bitcast(I32) for k in range(3))
        eL, mL, tL = (lin[:, k] for k in range(3))
        tabf, s1f = acc[:, 0, 0:NB], acc[:, 0, 64:64 + G]
        tab, s1p = (acc[:, 0, 256 + 128 * k:256 + 128 * k + 3 * 32].bitcast(BF16).rearrange("p (k b) -> p k b", k=3)[:, :, 0:NB]
                    for k in range(2))
        s1w = acc[:, 0, 512:512 + 3 * 64].bitcast(BF16).rearrange("p (k b) -> p k b", k=3)[:, :, 0:G]
        s1rows = acc[0:NB, 0, 1024:1024 + 3 * P // 2].bitcast(BF16).rearrange("a (k p) -> a k p", k=3)
        prod = acc[:, 0, 6 * LW:6 * LW + GT * NB].rearrange("p (t a) -> p t a", a=NB)
        mask = acc[:, 0, 6 * LW + GT * NB:6 * LW + GT * NB + GT * NB // 2].bitcast(BF16).rearrange("p (t a) -> p t a", a=NB)
        sameL = sb("sameL", [LP, LW], BF16)
        penL = sb("penL", [LP, LW], BF16)
        penN = sb("penN", [LP, LW], BF16)
        srcC = sb("srcC", [P, TP], I32)
        hiC = sb("hiC", [P, TP], BF16)
        rankC = sb("rankC", [P, TP])
        ewC = sb("ewC", [P, TP])
        t2C = sb("t2C", [P, TP])
        eC = sb("eC", [P, TP])
        dmin = sb("dmin", [P, EB])
        base7 = sb("base7", [EB, 16])
        base7i = sb("base7i", [EB, 16], I32)
        baseB = sb("baseB", [P, EB * 16])
        base_row = sb("base_row", [1, EB * 16], I32)
        stage = sb("stage", [P, RT], I32)
        ring = sb("ring", [P, RT, D])
        S = sb("S", [P, 2, GT, W])
        SH = S[:, :, :, :].bitcast(BF16)
        ewS = sb("ewS", [P, 2, GT, 3], BF16)
        xsb = sb("xsb", [P, NB, D])
        x2T = sb("x2T", [P, NA])
        deg3 = x2T[0:3, :]
        dinv = sb("dinv", [P, NB])
        dtmp = sb("dtmp", [P, 2, NB])
        rh = sb("rh", [P, 2, GT, D])
        rhH = rh[:, :, :, :].rearrange("p a t d -> p (a t d)").bitcast(BF16)
        ewP = rhH[:, 0:TP * 3].rearrange("p (t k) -> p t k", k=3)
        fcw, fcrw, lw, a2B = (rh[:, 1, 4 + k, :] for k in range(4))
        loB, rankB = (rhH[:, k * 2 * GE:(k + 1) * 2 * GE].rearrange("p (a n) -> p a n", a=2) for k in range(2))
        S1 = S[:, :, :, :].rearrange("p a t w -> p (a t w)")
        ohL, ohR = (S1.bitcast(BF16)[:, k * 2 * GE:(k + 1) * 2 * GE].rearrange("p (a n) -> p a n", a=2) for k in range(2))
        u = S1[:, 0:NC * D].rearrange("p (b d) -> p b d", d=D)
        w1 = sb("w1", [P, D])
        w2 = sb("w2", [P, D])
        aw3 = sb("aw3", [3, D])
        awT = sb("awT", [P, 3])
        fcwT = sb("fcwT", [P, D])
        fcrwT = sb("fcrwT", [P, D])
        wz = sb("wz", [P, D])
        v01 = sb("v01", [P, 2])
        v2B = sb("v2B", [P, D])
        b1B = sb("b1B", [P, D])
        b2B = sb("b2B", [P, D])
        bst = sb("bst", [P, NC, 6])
        mv = sb("mv", [P, NC, 2])
        sd = sb("sd", [P, NC])
        rs = sb("rs", [P, NC])
        epsc = sb("epsc", [P, 1])
        selC = ewC
        ends = 6 * LW + 2 * GT * NB
        lend, lini = acc[:, 0, ends:ends + 2], acc[:, 0, ends + 2:ends + 3]
        lrow = acc[0:1, 0, ends + 4:ends + 4 + 2 * P].rearrange("a (k p) -> a k p", k=2)
        lcar = acc[0:1, 0, ends + 4 + 2 * P:ends + 6 + 3 * P]

        ps = [ctx.enter_context(nc.psum_tensor(f"ps{k}", [P, 512], FP32)) for k in range(8)]

        sems = {}

        def s(name):
            if name not in sems:
                sems[name] = sem(name)
            return sems[name]

        gathered = [sem(f"gathered{j}") for j in range(RG)]
        rh_loaded = [sem(f"rh_loaded{j}") for j in range(2)]
        lo_loaded = [sem(f"lo_loaded{j}") for j in range(2)]
        block = ctx.enter_context(nc.Block())

        def ecols(q, n=GT):
            return bass.ds(q * GT, n)

        def erows(ap, first, n):
            return ap[first * P:(first + n) * P].rearrange("(t p) -> t p", p=P)

        @block.sync
        def _(sp):
            sp.wait_ge(s("pads_set"), 6)
            for dram, tile in ((dst, dstR), (edge_weight, ewR), (src, srcR)):
                for b in range(EB - 1):
                    sp.dma_start(tile[:, b, :], erows(dram, b * P, P)).then_inc(s("edges_loaded"), 16)
                rest = FT - (EB - 1) * P
                sp.dma_start(tile[0:rest, EB - 1, :], erows(dram, (EB - 1) * P, rest)).then_inc(s("edges_loaded"), 16)
                sp.dma_start(tile[rest:rest + 1, EB - 1, 0:FR],
                             dram[FT * P:E].rearrange("(a n) -> a n", a=1)).then_inc(s("edges_loaded"), 16)
            for tile, p0, p1, j0, j1, e0 in ((dL, 0, LP, 0, LW, 0), (dprevL, 0, 1, 1, LW, 0), (dprevL, 1, LP, 0, LW, LW - 1),
                                             (dnextL, 0, LP - 1, 0, LW, 1), (dnextL, LP - 1, LP, 0, LW - 1, E - LW + 1)):
                n = (p1 - p0) * (j1 - j0)
                sp.dma_start(tile[p0:p1, j0:j1], dst[e0:e0 + n].rearrange("(p j) -> p j", p=p1 - p0)
                             ).then_inc(s("lin_loaded"), 16)
            for b in range(0, NB - 1, 8):
                sp.dma_start(xsb[:, b:b + 8, :], x[b * P:(b + 8) * P, :].rearrange("(b p) d -> p b d", p=P)
                             ).then_inc(s("x_loaded"), 16)
            sp.dma_start(xsb[0:NLAST, NB - 1, :], x[(NB - 1) * P:N, :]).then_inc(s("x_loaded"), 16)
            for dram, tile in ((W1, w1), (W2, w2), (fc_w, fcw), (fc_r_w, fcrw), (loop_w, lw)):
                sp.dma_start(tile[:, :], dram[:, :]).then_inc(s("weights_loaded"), 16)
            sp.dma_start(aw3[:, :], attn_w.rearrange("a (k d) -> (a k) d", k=3)).then_inc(s("weights_loaded"), 16)
            for dram, tile in ((b1, b1B), (b2, b2B)):
                sp.dma_start(tile[:, :], dram.rearrange("(a d) -> a d", a=1).broadcast_to([P, D])
                             ).then_inc(s("weights_loaded"), 16)
            sp.wait_ge(s("base_made"), 2)
            sp.dma_start(basef_d.rearrange("(a g) -> a g", g=16), base7[:, :]).then_inc(s("base_stored"), 16)
            sp.dma_start(basei_d.rearrange("(a g) -> a g", g=16), base7i[:, :]).then_inc(s("base_stored"), 16)
            sp.wait_ge(s("base_stored"), 32)
            sp.dma_start(baseB[:, :], basef_d.rearrange("(a g) -> a g", a=1).broadcast_to([P, EB * 16])
                         ).then_inc(s("base_loaded"), 16)
            sp.dma_start(base_row[:, :], basei_d.rearrange("(a g) -> a g", a=1)).then_inc(s("base_loaded"), 16)
            sp.wait_ge(s("lo_made"), 1)
            sp.dma_start(lo_d.rearrange("(b t p) -> t b p", t=P, p=P), loH[:, :, :]).then_inc(s("lo_stored"), 16)
            sp.wait_ge(s("rank_rows"), 2)
            sp.dma_start(rank_d.rearrange("(b t p) -> t b p", t=P, p=P), loH[:, :, :]).then_inc(s("lo_stored"), 16)

            def store_chunks(table, made, stored, rows=rows):
                with sp.Fori(0, NCH) as c:
                    sp.wait_ge(made, c + 1)
                    sp.dma_start(table[bass.ds(c * NC * P, NC * P), :].rearrange("(b p) d -> p b d", p=P),
                                 rows[:, bass.ds(c * NC, NC), :]).then_inc(stored, 16)

            store_chunks(x1_d, s("x1_made"), s("x1_stored"))

            def load_rh(q, slot, n=GT):
                sp.dma_start(rh[:, slot, 0:n, :], edge_attr[bass.ds(q * GE, n * P), :].rearrange("(t p) d -> p t d", p=P)
                             ).then_inc(rh_loaded[slot], 16)

            def load_all_rh(used, base, tails):
                for j in range(2):
                    load_rh(j, j)
                with sp.Fori(1, G // 2 - 1) as i:
                    for j in range(2):
                        sp.wait_ge(used, i * 2 + (j - 1 + base))
                        load_rh(i * 2 + j, j)
                sp.wait_ge(used, base + G - 3)
                load_rh(G - 2, 0)
                sp.wait_ge(used, base + G - 2)
                sp.dma_start(rh[0:FR, 1, FT - (G - 1) * GT, :], edge_attr[FT * P:E, :]).then_inc(s("tail_loaded"), 16)
                sp.wait_ge(s("tail_loaded"), 16 * tails)
                load_rh(G - 1, 1, FT - (G - 1) * GT)

            store_chunks(h1_d, s("h1_made"), s("h1_stored"))
            load_all_rh(s("rh_dotted"), 0, 1)
            store_chunks(x2_d, s("x2_made"), s("x2_stored"), xsb)
            sp.wait_ge(s("s1_rows"), 1)
            sp.dma_start(s1_d[:, :].rearrange("k (a p) -> a k p", p=P), s1rows[:, :, :]).then_inc(s("s1_stored"), 16)
            sp.wait_ge(s("s1_stored"), 16)
            sp.wait_ge(s("s1_cleared"), 1)
            sp.dma_start(s1P[0:3, 0:NB * P], s1_d[:, :]).then_inc(s("s1_loaded"), 16)
            sp.wait_ge(s("lo_stored"), 32)
            def load_lo(q, slot):
                for dram, tile in ((lo_d, loB), (rank_d, rankB)):
                    sp.dma_start(tile[:, slot, :], dram[bass.ds(q * GE, GE)].rearrange("(a n) -> a n", a=1)
                                 .broadcast_to([P, GE])).then_inc(lo_loaded[slot], 16)
            for j in range(2):
                load_lo(j, j)
            with sp.Fori(1, G // 2 + 1) as i:
                for j in range(2):
                    sp.wait_ge(s("onehot_built"), i * 2 + (j - 1))
                    load_lo(i * 2 + j, j)
            sp.wait_ge(s("e_rows"), 2)
            sp.dma_start(e_d.rearrange("(b t p) -> t b p", t=P, p=P), rowF[:, 0, :, :]).then_inc(s("e_stored"), 16)
            sp.wait_ge(s("e_stored"), 16)
            sp.dma_start(eL, e_d[0:E].rearrange("(p j) -> p j", p=LP)).then_inc(s("e_loaded"), 16)
            sp.wait_ge(s("alpha_made"), 1)
            sp.dma_start(al_d.rearrange("(p j) -> p j", p=LP), mL).then_inc(s("alpha_stored"), 16)
            sp.wait_ge(s("alpha_stored"), 16)
            for b in range(EB - 1):
                sp.dma_start(rowF[:, 0, b, :], erows(al_d, b * P, P)).then_inc(s("alpha_loaded"), 16)
            sp.dma_start(rowF[0:rest, 0, EB - 1, :], erows(al_d, (EB - 1) * P, rest)).then_inc(s("alpha_loaded"), 16)
            sp.dma_start(rowF[rest:rest + 1, 0, EB - 1, 0:FR], al_d[FT * P:E].rearrange("(a n) -> a n", a=1)
                         ).then_inc(s("alpha_loaded"), 16)
            load_all_rh(s("summed"), 2 * G, 2)
            with sp.Fori(0, NCH - 1) as c:
                sp.wait_ge(s("out_made"), c + 2)
                sp.dma_start(out[bass.ds(c * NC * P, NC * P), :].rearrange("(b p) d -> p b d", p=P),
                             xsb[:, bass.ds(c * NC, NC), :]).then_inc(s("out_stored"), 16)
            sp.wait_ge(s("out_made"), NCH + 1)
            sp.dma_start(out[(NCH - 1) * NC * P:(NB - 1) * P, :].rearrange("(b p) d -> p b d", p=P),
                         xsb[:, (NCH - 1) * NC:NB - 1, :]).then_inc(s("out_stored"), 16)
            sp.dma_start(out[(NB - 1) * P:N, :], xsb[0:NLAST, NB - 1, :]).then_inc(s("out_stored"), 16)
            sp.wait_ge(s("out_stored"), 16 * (NCH + 1))

        @block.gpsimd
        def _(pool):
            nc.gpsimd.memset(dstR[:, EB - 1, :], int(FAR)).then_inc(s("pads_set"), 1)
            nc.gpsimd.memset(ewR[:, EB - 1, :], 0.0).then_inc(s("pads_set"), 1)
            nc.gpsimd.memset(srcR[:, EB - 1, :], 0).then_inc(s("pads_set"), 1)
            nc.gpsimd.memset(xsb[:, NB - 1, :], 0.0).then_inc(s("pads_set"), 1)
            nc.gpsimd.memset(dprevL[:, 0:LW], -1).then_inc(s("pads_set"), 1)
            nc.gpsimd.memset(dnextL[:, 0:LW], -1).then_inc(s("pads_set"), 1)
            nc.gpsimd.iota(iota_i[:, :], [[1, P]], base=0, channel_multiplier=0).then_inc(s("iota_made"), 1)
            nc.gpsimd.iota(pidx_i[:, :], [[1, 1]], base=0, channel_multiplier=1).then_inc(s("iota_made"), 1)
            nc.gpsimd.memset(acc[:, 0, NB * P:NA], 0.0).then_inc(s("tails_set"), 1)
            nc.gpsimd.memset(x2T[:, :], 0.0).then_inc(s("tails_set"), 1)
            nc.gpsimd.memset(ones_h[:, :], 1.0).then_inc(s("tails_set"), 1)
            nc.gpsimd.memset(ones3[:, :], 1.0).then_inc(s("tails_set"), 1)
            nc.gpsimd.memset(epsc[:, :], EPS).then_inc(s("tails_set"), 1)

            def gather_pass(p, table):
                with pool.Fori(0, IT) as it:
                    for j in range(RG):
                        pool.wait_ge(s("staged"), it * RG + (p * G + j + 1))
                        pool.sem_inc(s("pool_passed"))
                        for k in range(GT):
                            c = j * GT + k
                            pool.indirect_dma_start(
                                ring[:, c, :], None, table[:, :],
                                bass.IndirectOffsetOnAxis(ap=stage[:, c:c + 1], axis=0)).then_inc(gathered[j], 16)

            pool.wait_ge(s("x1_stored"), 16 * NCH)
            gather_pass(0, x1_d)
            pool.wait_ge(s("h1_stored"), 16 * NCH)
            gather_pass(1, h1_d)
            nc.gpsimd.memset(s1P, 0.0).then_inc(s("s1_cleared"), 1)
            pool.wait_ge(s("x2_stored"), 16 * NCH)
            gather_pass(2, x2_d)

        @block.tensor
        def _(pe):
            nbatch = 0
            pe.wait_ge(s("ident_made"), 1)

            def rows_to_cols(tile, ready, count):
                nonlocal nbatch
                pe.wait_ge(ready, count)
                for h in range(2):
                    if nbatch >= 2:
                        pe.wait_ge(s("cols_copied"), nbatch - 1)
                    n = min(4, EB - 4 * h)
                    for b in range(n):
                        last = nc.tensor.transpose(ps[nbatch % 2][:, b * P:(b + 1) * P], tile[:, 4 * h + b, :], ident[:, :])
                    last.then_inc(s("cols_ready"), 1)
                    nbatch += 1

            pe.wait_ge(s("dmin_made"), 1)
            nc.tensor.transpose(ps[2][0:EB, 0:P], dmin[:, :], ident[:, :]).then_inc(s("dmin_turned"), 1)
            rows_to_cols(rowF[:, 0], s("rowF_made"), 1)
            rows_to_cols(ewR, s("edges_loaded"), 16 * 3 * (EB + 1))
            rows_to_cols(rowF[:, 1], s("rowF_made"), 2)
            rows_to_cols(rowF[:, 2], s("rowF_made"), 3)
            pe.wait_ge(s("weights_loaded"), 16 * 8)
            nc.tensor.transpose(ps[3][:, 0:P], fcw[:, :], ident[:, :])
            nc.tensor.transpose(ps[3][:, P:2 * P], fcrw[:, :], ident[:, :])
            nc.tensor.matmul(ps[3][:, 2 * P:3 * P], fcw[:, :], lw[:, :], start=True, stop=True)
            nc.tensor.transpose(ps[3][:, 3 * P:3 * P + 3], aw3[:, :], ident[0:3, 0:3]).then_inc(s("wprod"), 1)
            pe.wait_ge(s("awT_copied"), 2)
            nc.tensor.matmul(ps[4][:, 0:2], fcw[:, :], awT[:, 0:2], start=True, stop=True)
            nc.tensor.matmul(ps[4][:, P:2 * P], a2B[:, :], fcrw[:, :], start=True, stop=True).then_inc(s("wprod"), 1)
            pe.wait_ge(s("rank_made"), 1)
            for h in range(2):
                pe.wait_ge(s("cols_copied"), nbatch - 1)
                n = min(4, EB - 4 * h)
                for b in range(n):
                    last = nc.tensor.transpose(ps[nbatch % 2][:, b * P:(b + 1) * P],
                                               rankC[:, (4 * h + b) * P:(4 * h + b + 1) * P], ident[:, :])
                last.then_inc(s("cols_ready"), 1)
                nbatch += 1

            with pe.Fori(0, G // 2) as i:
                for j in range(2):
                    pe.wait_ge(s("deg_onehot"), i * 2 + (j + 1))
                    for k in range(GT):
                        last = nc.tensor.matmul(ps[5 + j][0:3, 0:W], ewS[:, j, k, :], SH[:, j, k, 0:W],
                                                start=(k == 0), stop=(k == GT - 1))
                    last.then_inc(s("deg_summed"), 1)
            pe.wait_ge(s("deg_state"), G + 1)
            for b in range(NB):
                last = nc.tensor.matmul(ps[7][:, b:b + 1], deg3[0:3, b * P:(b + 1) * P], ones3[0:3, 0:1],
                                        start=True, stop=True)
            last.then_inc(s("deg_cols"), 1)
            for c in range(NCH):
                pe.wait_ge(s("x1_made"), c + 1)
                for b in range(NC):
                    if b % 4 == 0:
                        pe.wait_ge(s("x1_evac"), c * 2 + (b // 4 + 1))
                    last = nc.tensor.transpose(ps[b // 4][:, (b % 4) * P:(b % 4 + 1) * P],
                                               rows[:, c * NC + b, :], ident[:, :])
                    if b in (3, NC - 1):
                        last.then_inc(s("x1_turned"), 1)

            def sum_pass(p):
                with pe.Fori(0, IT) as it:
                    for j in range(RG):
                        pe.wait_ge(gathered[j], it * (16 * GT) + 16 * GT * (p * IT + 1))
                        pe.wait_ge(s("S_built"), it * RG + (p * (G + 1) + j + 1))
                        for k in range(GT):
                            last = nc.tensor.matmul(ps[2 + j % 2][:, 0:W], ring[:, j * GT + k, :], S[:, j % 2, k, :],
                                                    start=(k == 0), stop=(k == GT - 1))
                        if p == 2:
                            pe.wait_ge(rh_loaded[j % 2], it * (8 * RG) + 16 * (G // 2 + j // 2 + 1))
                            for k in range(GT):
                                last = nc.tensor.matmul(ps[2 + j % 2][:, W:2 * W], rh[:, j % 2, k, :], S[:, j % 2, k, :],
                                                        start=(k == 0), stop=(k == GT - 1))
                        last.then_inc(s("summed"), 1)

            sum_pass(0)
            def layer(weight, ready, count, made, evac, turned, psA, rows=rows):
                pe.wait_ge(ready, count)
                for c in range(NCH):
                    for b in range(NC):
                        pe.wait_ge(psA[0], c * NC + (b + 1))
                        nc.tensor.matmul(ps[4 + b % 4][:, 0:D], acc[:, 0, (c * NC + b) * P:(c * NC + b + 1) * P], weight[:, :],
                                         start=True, stop=True).then_inc(psA[1], 1)
                    pe.wait_ge(made, c + 1)
                    for b in range(NC):
                        if b % 4 == 0:
                            pe.wait_ge(evac, c * 2 + (b // 4 + 1))
                        last = nc.tensor.transpose(ps[b // 4][:, (b % 4) * P:(b % 4 + 1) * P],
                                                   rows[:, c * NC + b, :], ident[:, :])
                        if b in (3, NC - 1):
                            last.then_inc(turned, 1)

            layer(w1, s("acc_added"), G + 1, s("h1_made"), s("h1_evac"), s("h1_turned"), (s("l1_free"), s("l1_prod")))
            sum_pass(1)
            layer(w2, s("acc_added"), 2 * G + 2, s("x2_made"), s("x2_evac"), s("x2_turned"), (s("l2_free"), s("l2_prod")), xsb)
            pe.wait_ge(s("x2_evac"), 2 * NCH + 2)
            for b in range(NB):
                last = nc.tensor.matmul(ps[6][:, 2 * b:2 * b + 2], x2T[:, b * P:(b + 1) * P], v01[:, :], start=True, stop=True)
            last.then_inc(s("scores"), 1)
            pe.wait_ge(s("tables_split"), 1)
            for part in range(3):
                last = nc.tensor.transpose(ps[1][0:NB, part * 64:(part + 1) * 64].bitcast(BF16), s1p[:, part, :], ident_h[:, :])
            last.then_inc(s("s1_turned"), 1)
            pe.wait_ge(s("s1_loaded"), 16)
            with pe.Fori(0, G // 2) as i:
                for j in range(2):
                    b = pe.value_load(base_row[0:1, bass.ds(i * 2 + j, 1)], min_val=0, max_val=N - 1)
                    last = nc.tensor.matmul(ps[7][:, bass.ds(i * 2 + j, 1)], s1P[:, bass.ds(b, W)], ones_h[:, :],
                                            start=True, stop=True)
                last.then_inc(s("windows"), 1)
            pe.wait_ge(s("tables_split"), 3)
            with pe.Fori(0, G // 2) as i:
                for j in range(2):
                    pe.wait_ge(s("onehot_built"), i * 2 + (j + 1))
                    for k in range(GT):
                        for part in range(3):
                            nc.tensor.matmul(ps[4 + j][:, 64 * k:64 * k + NB], ohL[:, j, k * P:(k + 1) * P], tab[:, part, :],
                                             start=(part == 0), stop=(part == 2))
                    for k in range(GT):
                        for part in range(3):
                            last = nc.tensor.matmul(ps[2 + j][:, k:k + 1], ohR[:, j, k * P:(k + 1) * P],
                                                    s1w[:, part, bass.ds(i * 2 + j, 1)], start=(part == 0), stop=(part == 2))
                    last.then_inc(s("looked_up"), 1)
            pe.wait_ge(s("e_cols"), 1)
            for h in range(2):
                n = min(4, EB - 4 * h)
                for b in range(n):
                    last = nc.tensor.transpose(ps[h][:, b * P:(b + 1) * P], eC[:, (4 * h + b) * P:(4 * h + b + 1) * P], ident[:, :])
                last.then_inc(s("e_turned"), 1)
            for n in range(4):
                pe.wait_ge(s("ends_made"), n + 1)
                nc.tensor.transpose(ps[6][0:1, 0:LP], lend[0:LP, 0:1], ident[0:LP, 0:LP])
                nc.tensor.transpose(ps[6][0:1, P:P + LP], lend[0:LP, 1:2], ident[0:LP, 0:LP]).then_inc(s("ends_turned"), 1)
                pe.wait_ge(s("carry_made"), n + 1)
                off = 2 if n % 2 else 0
                nc.tensor.transpose(ps[7][0:LP, 0:1], lcar[0:1, off:off + LP], ident[0:1, 0:1]).then_inc(s("carry_turned"), 1)
            pe.wait_ge(s("alpha_loaded"), 16 * (EB + 1))
            for h in range(2):
                n = min(4, EB - 4 * h)
                for b in range(n):
                    last = nc.tensor.transpose(ps[h][:, b * P:(b + 1) * P], rowF[:, 0, 4 * h + b, :], ident[:, :])
                last.then_inc(s("alpha_turned"), 1)
            sum_pass(2)
            pe.wait_ge(s("acc_added"), 3 * G + 3)
            for c in range(NCH):
                for b in range(NC):
                    pe.wait_ge(s("fin_free"), c * NC + (b + 1))
                    blk = slice((c * NC + b) * P, (c * NC + b + 1) * P)
                    nc.tensor.matmul(ps[4 + b % 4][:, 0:D], acc[:, 0, blk], fcwT[:, :], start=True, stop=False)
                    nc.tensor.matmul(ps[4 + b % 4][:, 0:D], acc[:, 1, blk], fcrwT[:, :], start=False, stop=False)
                    nc.tensor.matmul(ps[4 + b % 4][:, 0:D], x2T[:, blk], wz[:, :], start=False, stop=True
                                     ).then_inc(s("fin_prod"), 1)

        @block.scalar
        def _(act):
            act.wait_ge(s("deg_clamped"), 1)
            nc.scalar.activation(dtmp[:, 0, :], dtmp[:, 0, :], ACT.Sqrt).then_inc(s("deg_root"), 1)

            def evacuate(turned, count, evac, dest, col0, ready=None):
                with act.Fori(0, NCH) as c:
                    for h in range(2):
                        n = 4 if h == 0 else NC - 4
                        act.wait_ge(turned, c * 2 + (h + 1 + count))
                        act.sem_inc(s("act_passed"))
                        nc.scalar.copy(dest[:, bass.ds(c * (NC * P) + h * 4 * P, n * P)], ps[h][:, 0:n * P]
                                       ).then_inc(evac, 1)

            evacuate(s("x1_turned"), 0, s("x1_evac"), acc[:, 0, :], 0)
            evacuate(s("h1_turned"), 0, s("h1_evac"), acc[:, 0, :], 0)
            with act.Fori(0, NCH) as c:
                for b in range(NC):
                    act.wait_ge(s("l2_free"), c * NC + (b + 4))
                    nc.scalar.activation(u[:, b, :], u[:, b, :], ACT.Sigmoid).then_inc(s("l2_sigm"), 1)
                act.wait_ge(s("l2_stats"), c + 1)
                nc.scalar.activation(sd[:, :], mv[:, :, 1], ACT.Sqrt, bias=epsc[:, 0:1]).then_inc(s("l2_root"), 1)
                for h in range(2):
                    n = 4 if h == 0 else NC - 4
                    act.wait_ge(s("x2_turned"), c * 2 + (h + 1))
                    act.sem_inc(s("act_passed"))
                    nc.scalar.copy(x2T[:, bass.ds(c * (NC * P) + h * 4 * P, n * P)], ps[h][:, 0:n * P]
                                   ).then_inc(s("x2_evac"), 1)
            act.wait_ge(s("e_shifted"), 1)
            nc.scalar.activation(eL, eL, ACT.Exp).then_inc(s("e_exp"), 1)
            with act.Fori(0, NCH) as c:
                act.wait_ge(s("fin_stats"), c + 1)
                nc.scalar.activation(sd[:, :], mv[:, :, 1], ACT.Sqrt, bias=epsc[:, 0:1]).then_inc(s("fin_root"), 1)

        @block.vector
        def _(dve):
            v = nc.vector
            steps = [0]

            def link(ins):
                steps[0] += 1
                ins.then_inc(s("dve_step"), 1)
                dve.wait_ge(s("dve_step"), steps[0])

            dve.wait_ge(s("iota_made"), 2)
            link(v.tensor_copy(pidx[:, :], pidx_i[:, :]))
            v.tensor_copy(iota_h[:, :], iota_i[:, :])
            link(v.tensor_copy(iota[:, :], iota_i[:, :]))
            v.tensor_scalar(ident_h[:, :], iota[:, :], pidx[:, 0:1], None, ALU.is_equal)
            v.tensor_scalar(ident[:, :], iota[:, :], pidx[:, 0:1], None, ALU.is_equal).then_inc(s("ident_made"), 1)
            dve.wait_ge(s("edges_loaded"), 16 * 3 * (EB + 1))
            v.tensor_copy(rowF[:, 0], dstR).then_inc(s("rowF_made"), 1)
            dve.wait_ge(s("rowF_made"), 1)
            v.tensor_reduce(dmin[:, :], rowF[:, 0], AX.X, ALU.min).then_inc(s("dmin_made"), 1)
            v.tensor_copy(rowF[:, 1], srcR).then_inc(s("rowF_made"), 1)
            link(v.tensor_scalar(loI, srcR, P - 1, None, ALU.bitwise_and))
            v.tensor_copy(loH[:, :, :], loI).then_inc(s("lo_made"), 1)
            dve.wait_ge(s("lo_made"), 1)
            link(v.tensor_scalar(loI, srcR, 7, None, ALU.arith_shift_right))
            v.tensor_copy(rowF[:, 2], loI).then_inc(s("rowF_made"), 1)
            dve.wait_ge(s("dmin_turned"), 1)
            link(v.tensor_reduce(base7[:, :], ps[2][0:EB, 0:P].rearrange("a (g t) -> a g t", t=GT), AX.X, ALU.min))
            v.tensor_copy(base7i[:, :], base7[:, :]).then_inc(s("base_made"), 2)

            ncol = [0]

            def cols_from(dest):
                for h in range(2):
                    n = min(4, EB - 4 * h) * P
                    ncol[0] += 1
                    dve.wait_ge(s("cols_ready"), ncol[0])
                    last = v.tensor_copy(dest[:, 4 * P * h:4 * P * h + n], ps[(ncol[0] - 1) % 2][:, 0:n])
                    last.then_inc(s("cols_copied"), 1)

            cols_from(rankC)
            cols_from(ewC)
            cols_from(srcC)
            cols_from(hiC)
            dve.wait_ge(s("cols_copied"), ncol[0])
            v.tensor_copy(srcC[:, T:T + RT], srcC[:, 0:RT]).then_inc(s("wrapped"), 1)
            split_tmp = t2C[:, :]
            link(v.tensor_copy(ewP[:, :, 0], ewC[:, :]))
            link(v.tensor_tensor(split_tmp, ewC[:, :], ewP[:, :, 0], ALU.subtract))
            link(v.tensor_copy(ewP[:, :, 1], split_tmp))
            link(v.tensor_tensor(split_tmp, split_tmp, ewP[:, :, 1], ALU.subtract))
            link(v.tensor_copy(ewP[:, :, 2], split_tmp))
            dve.wait_ge(s("lin_loaded"), 16 * 5)
            v.tensor_tensor(penN[:, :], dL, dnextL, ALU.is_equal)
            link(v.tensor_tensor(sameL[:, :], dL, dprevL, ALU.is_equal))
            link(v.tensor_scalar(penL[:, :], sameL[:, :], -1.0, BIG, ALU.add, ALU.mult))
            link(v.tensor_scalar(penN[:, :], penN[:, :], -1.0, BIG, ALU.add, ALU.mult))
            dve.wait_ge(s("base_loaded"), 32)
            rk = rankC[:, :].rearrange("p (g t) -> p g t", t=GT)
            v.tensor_tensor(rk, rk, baseB[:, :].unsqueeze(2).broadcast_to([P, EB * 16, GT]), ALU.subtract
                            ).then_inc(s("rank_made"), 1)
            dve.wait_ge(s("wprod"), 1)
            v.tensor_copy(fcwT[:, :], ps[3][:, 0:P])
            v.tensor_copy(fcrwT[:, :], ps[3][:, P:2 * P])
            v.tensor_copy(wz[:, :], ps[3][:, 2 * P:3 * P])
            v.tensor_copy(awT[:, :], ps[3][:, 3 * P:3 * P + 3]).then_inc(s("awT_copied"), 1)
            dve.wait_ge(s("awT_copied"), 1)
            v.tensor_copy(a2B[:, :], awT[:, 2:3].broadcast_to([P, P])).then_inc(s("awT_copied"), 1)
            dve.wait_ge(s("wprod"), 2)
            v.tensor_copy(v01[:, :], ps[4][:, 0:2])
            v.tensor_copy(v2B[:, :], ps[4][:, P:2 * P]).then_inc(s("v_made"), 1)
            dve.wait_ge(s("lo_stored"), 16)
            for h in range(2):
                ncol[0] += 1
                n = min(4, EB - 4 * h)
                dve.wait_ge(s("cols_ready"), ncol[0])
                v.tensor_copy(loH[:, 4 * h:4 * h + n, :], ps[(ncol[0] - 1) % 2][:, 0:n * P].rearrange("p (b t) -> p b t", t=P)
                              ).then_inc(s("rank_rows"), 1)

            dve.wait_ge(s("rank_made"), 1)
            dve.wait_ge(s("tails_set"), 5)

            def deg_onehot(q, slot):
                v.tensor_copy(ewS[:, slot, :, :], ewP[:, ecols(q), :])
                for k in range(GT):
                    last = v.tensor_scalar(SH[:, slot, k, 0:W], iota_h[:, :], rankC[:, bass.ds(q * GT + k, 1)], None, ALU.is_equal)
                last.then_inc(s("deg_onehot"), 1)

            deg_onehot(0, 0)
            v.tensor_copy(stage[:, :], srcC[:, 0:RT]).then_inc(s("staged"), RG)
            dve.sem_inc(s("deg_state"), 1)
            with dve.Fori(0, G // 2) as i:
                for j in range(2):
                    deg_onehot(i * 2 + (j + 1), (j + 1) % 2)
                    b = dve.value_load(base_row[0:1, bass.ds(i * 2 + j, 1)], min_val=0, max_val=N - 1)
                    win = deg3[:, bass.ds(b, W)]
                    dve.wait_ge(s("deg_state"), i * 2 + (j + 1))
                    dve.wait_ge(s("deg_summed"), i * 2 + (j + 1))
                    ins = v.tensor_tensor(win, ps[5 + j][0:3, 0:W], win, ALU.add)
                    ins.then_inc(s("deg_state"), 1)
            dve.wait_ge(s("deg_cols"), 1)
            link(v.tensor_scalar(dinv[:, :], ps[7][:, 0:NB], 1.0, None, ALU.add))
            v.tensor_scalar(dtmp[:, 0, :], dinv[:, :], 1e-30, None, ALU.max).then_inc(s("deg_clamped"), 1)
            link(v.tensor_scalar(dtmp[:, 1, :], dinv[:, :], 0.0, None, ALU.is_gt))
            dve.wait_ge(s("deg_root"), 1)
            link(v.reciprocal(dtmp[:, 0, :], dtmp[:, 0, :]))
            link(v.tensor_tensor(dinv[:, :], dtmp[:, 0, :], dtmp[:, 1, :], ALU.mult))
            dve.wait_ge(s("x_loaded"), 16 * 7)
            dve.sem_inc(s("x1_evac"), 2)
            with dve.Fori(0, NCH) as c:
                for b in range(NC):
                    last = v.tensor_scalar(rows[:, c * NC + b, :], xsb[:, c * NC + b, :],
                                           dinv[:, bass.ds(c * NC + b, 1)], None, ALU.mult)
                last.then_inc(s("x1_made"), 1)

            def build_S(q, slot, wcols):
                for k in range(GT):
                    col = bass.ds(q * GT + k, 1)
                    last = v.tensor_scalar(S[:, slot, k, :], iota[:, :], rankC[:, col], wcols[:, col], ALU.is_equal, ALU.mult)
                last.then_inc(s("S_built"), 1)

            def edge_pass(p, wcols, extra=None):
                naccs = 2 if p == 2 else 1
                build_S(0, 0, wcols)
                with dve.Fori(0, IT) as it:
                    for j in range(RG):
                        q = it * RG + j
                        build_S(q + 1, (j + 1) % 2, wcols)
                        if extra:
                            extra(q, it, j)
                        b = dve.value_load(base_row[0:1, bass.ds(q, 1)], min_val=0, max_val=N - 1)
                        win = acc[:, 0:naccs, bass.ds(b, W)]
                        dve.wait_ge(s("acc_added"), it * RG + (p * (G + 1) + j + 1))
                        dve.wait_ge(s("summed"), it * RG + (p * G + j + 1))
                        v.tensor_tensor(win, ps[2 + j % 2][:, 0:naccs * W].rearrange("p (a w) -> p a w", a=naccs), win, ALU.add
                                        ).then_inc(s("acc_added"), 1)
                        v.tensor_copy(stage[:, j * GT:(j + 1) * GT], srcC[:, ecols(q + RG)]).then_inc(s("staged"), 1)

            dve.wait_ge(s("x1_evac"), 2 * NCH + 2)
            dve.sem_inc(s("acc_added"), 1)
            edge_pass(0, ewC)
            dve.wait_ge(s("acc_added"), G + 1)
            dve.sem_inc(s("l1_free"), 3)
            dve.sem_inc(s("h1_evac"), 2)
            dve.wait_ge(s("x1_stored"), 16 * NCH)
            with dve.Fori(0, NCH) as c:
                for b in range(NC):
                    col = bass.ds(c * NC + b, 1)
                    dve.wait_ge(s("l1_prod"), c * NC + (b + 1))
                    v.scalar_tensor_tensor(u[:, b, :], ps[4 + b % 4][:, 0:D], dinv[:, col], b1B[:, :], ALU.mult, ALU.add
                                           ).then_inc(s("l1_free"), 1)
                for b in range(NC):
                    dve.wait_ge(s("l1_free"), c * NC + (b + 4))
                    last = v.tensor_scalar(rows[:, c * NC + b, :], u[:, b, :], 0.0, dinv[:, bass.ds(c * NC + b, 1)], ALU.max, ALU.mult)
                last.then_inc(s("h1_made"), 1)

            def dots(q, it, j):
                dve.wait_ge(rh_loaded[j % 2], it * (16 * RG // 2) + (16 * (j // 2 + 1)))
                dve.sem_inc(s("dve_passed"))
                for k in range(GT):
                    last = v.scalar_tensor_tensor(rh[:, j % 2, k, :], rh[:, j % 2, k, :], 1.0, v2B[:, :], ALU.mult, ALU.mult,
                                                  accum_out=t2C[:, bass.ds(q * GT + k, 1)])
                last.then_inc(s("rh_dotted"), 1)

            dve.wait_ge(s("h1_evac"), 2 * NCH + 2)
            dve.sem_inc(s("acc_added"), 1)
            edge_pass(1, ewC, dots)

            dve.wait_ge(s("acc_added"), 2 * G + 2)
            dve.sem_inc(s("l2_free"), 3)
            dve.sem_inc(s("x2_evac"), 2)
            dve.wait_ge(s("h1_stored"), 16 * NCH)
            with dve.Fori(0, NCH) as c:
                for b in range(NC):
                    col = bass.ds(c * NC + b, 1)
                    dve.wait_ge(s("l2_prod"), c * NC + (b + 1))
                    v.scalar_tensor_tensor(u[:, b, :], ps[4 + b % 4][:, 0:D], dinv[:, col], b2B[:, :], ALU.mult, ALU.add
                                           ).then_inc(s("l2_free"), 1)
                for b in range(NC):
                    dve.wait_ge(s("l2_sigm"), c * NC + (b + 1))
                    v.tensor_tensor(u[:, b, :], u[:, b, :], xsb[:, c * NC + b, :], ALU.add).then_inc(s("l2_res"), 1)
                for b in range(NC):
                    dve.wait_ge(s("l2_res"), c * NC + (b + 1))
                    v.bn_stats(bst[:, b, :], u[:, b, :]).then_inc(s("l2_bn"), 1)
                dve.wait_ge(s("l2_bn"), c * NC + NC)
                dve.sem_inc(s("dve_passed"))
                for b in range(NC):
                    last = v.bn_aggr(mv[:, b, :], bst[:, b, :])
                last.then_inc(s("l2_stats"), 1)
                dve.wait_ge(s("l2_root"), c + 1)
                v.reciprocal(rs[:, :], sd[:, :]).then_inc(s("l2_rs"), 1)
                dve.wait_ge(s("l2_rs"), c + 1)
                for b in range(NC):
                    last = v.tensor_scalar(xsb[:, c * NC + b, :], u[:, b, :], mv[:, b, 0:1], rs[:, b:b + 1], ALU.subtract, ALU.mult)
                last.then_inc(s("x2_made"), 1)

            def split3(parts, full, tmp):
                link(v.tensor_copy(parts[:, 0, :], full))
                link(v.tensor_tensor(tmp, full, parts[:, 0, :], ALU.subtract))
                link(v.tensor_copy(parts[:, 1, :], tmp))
                link(v.tensor_tensor(tmp, tmp, parts[:, 1, :], ALU.subtract))
                v.tensor_copy(parts[:, 2, :], tmp).then_inc(s("tables_split"), 1)

            dve.wait_ge(s("scores"), 1)
            score = ps[6][:, 0:2 * NB].rearrange("p (b k) -> p b k", k=2)
            v.tensor_copy(tabf[:, :], score[:, :, 0])
            link(v.tensor_copy(s1f[:, 0:NB], score[:, :, 1]))
            split3(s1p, s1f[:, 0:NB], dtmp[:, 0, :])
            split3(tab, tabf[:, :], dtmp[:, 1, :])
            dve.wait_ge(s("s1_turned"), 1)
            v.tensor_copy(s1rows[:, :, :], ps[1][0:NB, 0:3 * 64].bitcast(BF16).rearrange("a (k p) -> a k p", k=3)
                          ).then_inc(s("s1_rows"), 1)
            dve.wait_ge(s("windows"), G // 2)
            link(v.tensor_copy(s1f[:, :], ps[7][:, 0:G]))
            split3(s1w, s1f[:, :], selC[:, 0:G])

            def onehots(q, i, j):
                dve.wait_ge(lo_loaded[j], i * 32 + 32)
                v.tensor_scalar(ohL[:, j, :], loB[:, j, :], pidx[:, 0:1], None, ALU.is_equal)
                v.tensor_scalar(ohR[:, j, :], rankB[:, j, :], pidx[:, 0:1], None, ALU.is_equal).then_inc(s("onehot_built"), 1)

            onehots(0, 0, 0)
            with dve.Fori(0, G // 2) as i:
                for j in range(2):
                    q = i * 2 + j
                    onehots(q + 1, i + j, (j + 1) % 2)
                    v.tensor_tensor(mask[:, :, :], iota[:, 0:NB].unsqueeze(1).broadcast_to([P, GT, NB]),
                                    hiC[:, ecols(q)].unsqueeze(2).broadcast_to([P, GT, NB]), ALU.is_equal).then_inc(s("sel_step"), 1)
                    dve.wait_ge(s("looked_up"), i * 2 + (j + 1))
                    dve.wait_ge(s("sel_step"), i * 4 + (2 * j + 1))
                    v.tensor_tensor(prod[:, :, :], ps[4 + j][:, :].rearrange("p (k c) -> p k c", c=64)[:, :, 0:NB], mask[:, :, :], ALU.mult
                                    ).then_inc(s("sel_step"), 1)
                    v.tensor_tensor(eC[:, ecols(q)], ps[2 + j][:, 0:GT], t2C[:, ecols(q)], ALU.add)
                    dve.wait_ge(s("sel_step"), i * 4 + (2 * j + 2))
                    dve.sem_inc(s("dve_passed"))
                    last = v.tensor_reduce(selC[:, ecols(q)], prod[:, :, :], AX.X, ALU.add)
                last.then_inc(s("selected"), 1)
            dve.wait_ge(s("selected"), G // 2)
            v.memset(eC[:, T:TP], 0.0)
            link(v.tensor_tensor(eC[:, 0:T], eC[:, 0:T], selC[:, 0:T], ALU.add))
            v.scalar_tensor_tensor(eC[:, 0:T], eC[:, 0:T], SLOPE, eC[:, 0:T], ALU.mult, ALU.max).then_inc(s("e_cols"), 1)
            for h in range(2):
                n = min(4, EB - 4 * h)
                dve.wait_ge(s("e_turned"), h + 1)
                v.tensor_copy(rowF[:, 0, 4 * h:4 * h + n, :], ps[h][:, 0:n * P].rearrange("p (b t) -> p b t", t=P)).then_inc(s("e_rows"), 1)

            nscan = [0]

            def run_scan(out_, data, pen, op0, op1, neutral, reverse):
                n = nscan[0]
                nscan[0] += 1
                d, p_, o = (a[:, ::-1] if reverse else a for a in (data, pen, out_))
                v.tensor_tensor_scan(o, p_, d, neutral, op0, op1).then_inc(s("dve_step"), 1)
                steps[0] += 1
                link(v.tensor_reduce(lend[0:LP, 1:2], pen, AX.X, ALU.min))
                end = 0 if reverse else LW - 1
                v.tensor_copy(lend[0:LP, 0:1], out_[:, end:end + 1]).then_inc(s("ends_made"), 1)
                dve.wait_ge(s("ends_turned"), n + 1)
                link(v.tensor_copy(lrow[:, :, 0:LP], ps[6][0:1, 0:2 * P].rearrange("a (k p) -> a k p", k=2)[:, :, 0:LP]))
                link(v.memset(lcar[:, :], neutral))
                r0, r1, rc = lrow[0:1, 0, 0:LP], lrow[0:1, 1, 0:LP], lcar[0:1, 1:LP + 1]
                if reverse:
                    r0, r1, rc = r0[:, ::-1], r1[:, ::-1], rc[:, ::-1]
                v.tensor_tensor_scan(rc, r1, r0, neutral, op0, op1).then_inc(s("carry_made"), 1)
                dve.wait_ge(s("carry_turned"), n + 1)
                link(v.tensor_copy(lini[0:LP, :], ps[7][0:LP, 0:1]))
                link(v.tensor_tensor_scan(o, p_, d, lini[0:LP, 0:1], op0, op1))

            dve.wait_ge(s("e_loaded"), 16)
            run_scan(mL, eL, penL[:, :], ALU.add, ALU.max, -BIG, False)
            run_scan(tL, mL, penN[:, :], ALU.add, ALU.max, -BIG, True)
            v.tensor_tensor(eL, eL, tL, ALU.subtract).then_inc(s("e_shifted"), 1)
            dve.wait_ge(s("e_exp"), 1)
            run_scan(mL, eL, sameL[:, :], ALU.mult, ALU.add, 0.0, False)
            run_scan(tL, mL, penN[:, :], ALU.add, ALU.max, -BIG, True)
            link(v.reciprocal(tL, tL))
            link(v.memset(rowF[:, 0, EB - 1, :], 0.0))
            v.tensor_tensor(mL, eL, tL, ALU.mult).then_inc(s("alpha_made"), 1)
            for h in range(2):
                n = min(4, EB - 4 * h) * P
                dve.wait_ge(s("alpha_turned"), h + 1)
                link(v.tensor_copy(eC[:, 4 * P * h:4 * P * h + n], ps[h][:, 0:n]))
            v.memset(acc[:, :, :], 0.0).then_inc(s("acc_added"), 1)
            edge_pass(2, eC)

            dve.wait_ge(s("acc_added"), 3 * G + 3)
            dve.sem_inc(s("fin_free"), 3)
            dve.sem_inc(s("out_made"), 1)
            with dve.Fori(0, NCH) as c:
                dve.wait_ge(s("out_made"), c + 1)
                for b in range(NC):
                    dve.wait_ge(s("fin_prod"), c * NC + (b + 1))
                    v.scalar_tensor_tensor(u[:, b, :], ps[4 + b % 4][:, 0:D], 0.0, xsb[:, c * NC + b, :], ALU.max, ALU.add
                                           ).then_inc(s("fin_free"), 1)
                for b in range(NC):
                    dve.wait_ge(s("fin_free"), c * NC + (b + 4))
                    v.bn_stats(bst[:, b, :], u[:, b, :]).then_inc(s("fin_bn"), 1)
                dve.wait_ge(s("fin_bn"), c * NC + NC)
                dve.sem_inc(s("dve_passed"))
                for b in range(NC):
                    last = v.bn_aggr(mv[:, b, :], bst[:, b, :])
                last.then_inc(s("fin_stats"), 1)
                dve.wait_ge(s("fin_root"), c + 1)
                v.reciprocal(rs[:, :], sd[:, :]).then_inc(s("fin_rs"), 1)
                dve.wait_ge(s("fin_rs"), c + 1)
                for b in range(NC):
                    last = v.tensor_scalar(xsb[:, c * NC + b, :], u[:, b, :], mv[:, b, 0:1], rs[:, b:b + 1], ALU.subtract, ALU.mult)
                last.then_inc(s("out_made"), 1)


_INS = ['x', 'src', 'dst', 'edge_attr_128', 'edge_weight', 'L0_gnn_W1', 'L0_gnn_b1', 'L0_gnn_W2', 'L0_gnn_b2', 'L1_gnn_fc_w', 'L1_gnn_fc_r_w', 'L1_gnn_attn_w', 'L1_gnn_loop_w']
_OUTS = [((6250, 128), 'float32')]


def kernel(**inputs):
    import numpy as _np
    import concourse.bacc as _bacc
    from concourse import mybir as _mybir
    from concourse.bass_utils import run_bass_kernel_spmd as _run

    nc = _bacc.Bacc("TRN2", target_bir_lowering=False, num_devices=1)
    arrays, args = {}, []
    for name in _INS:
        a = _np.ascontiguousarray(inputs[name])
        arrays[f"in_{name}_dram"] = a
        args.append(nc.dram_tensor(f"in_{name}_dram", a.shape, _mybir.dt.from_np(a.dtype), kind="ExternalInput").ap())
    for i, (shape, dtype) in enumerate(_OUTS):
        dt = _mybir.dt.from_np(_np.dtype(dtype))
        args.append(nc.dram_tensor(f"out_{i}_dram", shape, dt, kind="ExternalOutput").ap())
    build(nc, *args)
    r = _run(nc, [arrays], core_ids=[0])
    got = tuple(r.results[0][f"out_{i}_dram"] for i in range(len(_OUTS)))
    return got[0]
```

```python
import concourse.bass as bass
from concourse import mybir
from contextlib import ExitStack

FP32 = mybir.dt.float32
BF16 = mybir.dt.bfloat16
I32 = mybir.dt.int32
ALU = mybir.AluOpType
ACT = mybir.ActivationFunctionType
AX = mybir.AxisListType

N, E, D = 6250, 100000, 128
P = 128
W = 128
GT = 8
GE = GT * P
G = -(-E // GE)
T = G * GT
EB = -(-T // P)
TP = EB * P
HG = G // 2
UG = 14
IT = G // UG
RG = 7
RTN = G // RG
RT = RG * GT
BACK = (0, 1, 2, 0, 1, 2, 3)
NBACK = max(BACK) + 1
RHS = (0, 1, 2, 3, 4) * 2 + (0, 1, 2, 3)
NRH = max(RHS) + 1
RS = RG + NBACK + NRH - 2
CREDIT = 16
NB = -(-N // P)
NC = 7
NCH = NB // NC
NLAST = N - (NB - 1) * P
NA = NB * P + W
FT = E // P
REST = FT - (EB - 1) * P
FR = E - FT * P
LP, LW = 125, 800
FAR = float(1 << 20)
BIG = 1.0e30
EPS = 1.0e-5
SLOPE = 0.01
assert G * GE == T * P and IT * UG == G and 2 * RG == UG and HG == RG * IT and TP - T >= RT and NCH * NC == NB and LP * LW == E


def build(nc, x, src, dst, edge_attr, edge_weight, W1, b1, W2, b2, fc_w, fc_r_w, attn_w, loop_w, out):
    ctx = ExitStack()
    with ctx:
        def sb(name, shape, dt=FP32):
            return ctx.enter_context(nc.sbuf_tensor(name, shape, dt))

        def sem(name):
            return ctx.enter_context(nc.semaphore(name))

        def scratch(name, shape, dt=FP32):
            return nc.dram_tensor(name, shape, dt).ap()

        parked_d = scratch("parked_d", (HG, P, GT * D))
        h1_d = scratch("h1_d", (NB * P, D))
        x2_d = scratch("x2_d", (NB * P, D))
        lo_d = scratch("lo_d", (TP * P,), BF16)
        rank_d = scratch("rank_d", (TP * P,), BF16)
        basef_d = scratch("basef_d", (EB * 16,))
        basei_d = scratch("basei_d", (EB * 16,), I32)
        s1_d = scratch("s1_d", (3, NB * P), BF16)
        e_d = scratch("e_d", (TP * P,))
        al_d = scratch("al_d", (E,))

        iota_i = sb("iota_i", [P, P], I32)
        pidx_i = sb("pidx_i", [P, 1], I32)
        iota = sb("iota", [P, P])
        iota_h = sb("iota_h", [P, P], BF16)
        pidx = sb("pidx", [P, 1])
        ident = sb("ident", [P, P])
        ident_h = sb("ident_h", [P, P], BF16)
        ones_h = sb("ones_h", [P, 1], BF16)
        ones3 = sb("ones3", [3, 1])
        acc = sb("acc", [P, 2, NA])
        rows = acc[:, 1, 0:NB * D].rearrange("p (b d) -> p b d", d=D)
        erow = acc[:, 1, 0:7 * TP].rearrange("p (a b t) -> p a b t", a=7, t=P)
        srcR, dstR, loI = (erow[:, k].bitcast(I32) for k in range(3))
        ewR, rowF = erow[:, 3], erow[:, 4:7]
        s1P = acc[:, 1, 0:NA // 2].bitcast(BF16)
        loH = sb("loH", [P, EB, P], BF16)
        lin = acc[0:LP, 0, 0:6 * LW].rearrange("p (k j) -> p k j", k=6)
        dL, dprevL, dnextL = (lin[:, k].bitcast(I32) for k in range(3))
        eL, mL, tL = (lin[:, k] for k in range(3))
        tabf, s1f = acc[:, 0, 0:NB], acc[:, 0, 64:64 + G]
        s1p = acc[:, 0, 256:256 + 3 * 32].bitcast(BF16).rearrange("p (k b) -> p k b", k=3)[:, :, 0:NB]
        s1w = acc[:, 0, 512:512 + 3 * 64].bitcast(BF16).rearrange("p (k b) -> p k b", k=3)[:, :, 0:G]
        s1rows = acc[0:NB, 0, 1024:1024 + 3 * P // 2].bitcast(BF16).rearrange("a (k p) -> a k p", k=3)
        tab = acc[:, 1, 5400:5400 + 3 * 32].bitcast(BF16).rearrange("p (k b) -> p k b", k=3)[:, :, 0:NB]
        prod = acc[:, 1, 5500:5500 + GT * NB].rearrange("p (t a) -> p t a", a=NB)
        sameL = sb("sameL", [LP, LW], BF16)
        penL = sb("penL", [LP, LW], BF16)
        penN = sb("penN", [LP, LW], BF16)
        srcC = sb("srcC", [P, TP], I32)
        hiC = sb("hiC", [P, TP])
        rankC = sb("rankC", [P, TP])
        ewC = sb("ewC", [P, TP])
        t2C = sb("t2C", [P, TP])
        eC = t2C
        dmin = sb("dmin", [P, EB])
        base7 = sb("base7", [EB, 16])
        base7i = sb("base7i", [EB, 16], I32)
        baseB = sb("baseB", [P, EB * 16])
        base_row = sb("base_row", [1, EB * 16], I32)
        stage = sb("stage", [P, 2, RT], I32)
        ring = sb("ring", [P, RS, GT, D])
        S = sb("S", [P, 2, GT, W])
        SH = S[:, :, :, :].bitcast(BF16)
        ewS = sb("ewS", [P, 2, GT, 3], BF16)
        xsb = sb("xsb", [P, NB, D])
        x2T = sb("x2T", [P, NA])
        deg3 = x2T[0:3, :]
        dinv = sb("dinv", [P, NB])
        dtmp = sb("dtmp", [P, 2, NB])
        rh = sb("rh", [P, 2, GT, D])
        rhH = rh[:, :, :, :].rearrange("p a t d -> p (a t d)").bitcast(BF16)
        ewP = rhH[:, 0:TP * 3].rearrange("p (t k) -> p t k", k=3)
        fcw, fcrw, lw, a2B = (rh[:, 1, 4 + k, :] for k in range(4))
        loB, rankB = (rhH[:, k * 2 * GE:(k + 1) * 2 * GE].rearrange("p (a n) -> p a n", a=2) for k in range(2))
        S1 = S[:, :, :, :].rearrange("p a t w -> p (a t w)")
        ohL, ohR = (S1.bitcast(BF16)[:, k * 2 * GE:(k + 1) * 2 * GE].rearrange("p (a n) -> p a n", a=2) for k in range(2))
        u = S1[:, 0:NC * D].rearrange("p (b d) -> p b d", d=D)
        w1 = sb("w1", [P, D])
        w2 = sb("w2", [P, D])
        aw3 = sb("aw3", [3, D])
        awT = sb("awT", [P, 3])
        fcwT = sb("fcwT", [P, D])
        fcrwT = sb("fcrwT", [P, D])
        wz = sb("wz", [P, D])
        v01 = sb("v01", [P, 2])
        v2B = sb("v2B", [P, D])
        b1B = sb("b1B", [P, D])
        b2B = sb("b2B", [P, D])
        bst = sb("bst", [P, NC, 6])
        mv = sb("mv", [P, NC, 2])
        sd = sb("sd", [P, NC])
        rs = sb("rs", [P, NC])
        epsc = sb("epsc", [P, 1])
        selC = ewC
        ends = 6 * LW
        lend, lini = acc[:, 0, ends:ends + 2], acc[:, 0, ends + 2:ends + 3]
        lrow = acc[0:1, 0, ends + 4:ends + 4 + 2 * P].rearrange("a (k p) -> a k p", k=2)
        lcar = acc[0:1, 0, ends + 4 + 2 * P:ends + 6 + 3 * P]

        ps = [ctx.enter_context(nc.psum_tensor(f"ps{k}", [P, 512], FP32)) for k in range(8)]

        sems = {}

        def s(name):
            if name not in sems:
                sems[name] = sem(name)
            return sems[name]

        rhv = [rh[:, 0], rh[:, 1]] + [ring[:, RG + NBACK + k] for k in range(NRH - 2)]
        gathered = [sem(f"gathered{j}") for j in range(RG)]
        parked = [sem(f"parked{j}") for j in range(RG)]
        reloaded = [sem(f"reloaded{j}") for j in range(RG)]
        rh_loaded = [sem(f"rh_loaded{j}") for j in range(2)]
        rh2_loaded = [sem(f"rh2_loaded{j}") for j in range(UG)]
        lo_loaded = [sem(f"lo_loaded{j}") for j in range(2)]
        rank_loaded = [sem(f"rank_loaded{j}") for j in range(2)]
        block = ctx.enter_context(nc.Block())

        def summed_by(p, n):
            return CREDIT + p * G + n

        def group(p, it, j):
            if p == 1:
                return it * UG + j, j % RG
            pair, fresh = divmod(j, 2)
            return it * RG + (pair + HG * fresh), pair if fresh else RG + BACK[pair % RG]

        def last_use(seq, j):
            return next(d for d in range(1, len(seq) + 1) if seq[(j - d) % len(seq)] == seq[j])

        def ecols(q, n=GT):
            return bass.ds(q * GT, n)

        def erows(ap, first, n):
            return ap[first * P:(first + n) * P].rearrange("(t p) -> t p", p=P)

        @block.sync
        def _(sp):
            sp.wait_ge(s("pads_set"), 6)
            for dram, tile, loaded in ((src, srcR, s("src_loaded")), (dst, dstR, s("dst_loaded")), (edge_weight, ewR, s("ew_loaded"))):
                for b in range(EB - 1):
                    sp.dma_start(tile[:, b, :], erows(dram, b * P, P)).then_inc(loaded, 16)
                sp.dma_start(tile[0:REST, EB - 1, :], erows(dram, (EB - 1) * P, REST)).then_inc(loaded, 16)
                sp.dma_start(tile[REST:REST + 1, EB - 1, 0:FR],
                             dram[FT * P:E].rearrange("(a n) -> a n", a=1)).then_inc(loaded, 16)
            for tile, p0, p1, j0, j1, e0 in ((dL, 0, LP, 0, LW, 0), (dprevL, 0, 1, 1, LW, 0), (dprevL, 1, LP, 0, LW, LW - 1),
                                             (dnextL, 0, LP - 1, 0, LW, 1), (dnextL, LP - 1, LP, 0, LW - 1, E - LW + 1)):
                n = (p1 - p0) * (j1 - j0)
                sp.dma_start(tile[p0:p1, j0:j1], dst[e0:e0 + n].rearrange("(p j) -> p j", p=p1 - p0)
                             ).then_inc(s("lin_loaded"), 16)
            for b in range(0, NB - 1, 8):
                sp.dma_start(xsb[:, b:b + 8, :], x[b * P:(b + 8) * P, :].rearrange("(b p) d -> p b d", p=P)
                             ).then_inc(s("x_loaded"), 16)
            sp.dma_start(xsb[0:NLAST, NB - 1, :], x[(NB - 1) * P:N, :]).then_inc(s("x_loaded"), 16)
            for dram, tile in ((W1, w1), (W2, w2), (fc_w, fcw), (fc_r_w, fcrw), (loop_w, lw)):
                sp.dma_start(tile[:, :], dram[:, :]).then_inc(s("weights_loaded"), 16)
            sp.dma_start(aw3[:, :], attn_w.rearrange("a (k d) -> (a k) d", k=3)).then_inc(s("weights_loaded"), 16)
            for dram, tile in ((b1, b1B), (b2, b2B)):
                sp.dma_start(tile[:, :], dram.rearrange("(a d) -> a d", a=1).broadcast_to([P, D])
                             ).then_inc(s("weights_loaded"), 16)
            sp.wait_ge(s("base_made"), 2)
            sp.dma_start(basef_d.rearrange("(a g) -> a g", g=16), base7[:, :]).then_inc(s("base_stored"), 16)
            sp.dma_start(basei_d.rearrange("(a g) -> a g", g=16), base7i[:, :]).then_inc(s("base_stored"), 16)
            sp.wait_ge(s("base_stored"), 32)
            sp.dma_start(baseB[:, :], basef_d.rearrange("(a g) -> a g", a=1).broadcast_to([P, EB * 16])
                         ).then_inc(s("base_loaded"), 16)
            sp.dma_start(base_row[:, :], basei_d.rearrange("(a g) -> a g", a=1)).then_inc(s("base_loaded"), 16)
            sp.wait_ge(s("lo_made"), 1)
            sp.dma_start(lo_d.rearrange("(b t p) -> t b p", t=P, p=P), loH[:, :, :]).then_inc(s("lo_stored"), 16)
            sp.wait_ge(s("rank_rows"), 2)
            sp.dma_start(rank_d.rearrange("(b t p) -> t b p", t=P, p=P), loH[:, :, :]).then_inc(s("lo_stored"), 16)

            def store_chunks(table, made, stored, rows=rows):
                with sp.Fori(0, NCH) as c:
                    sp.wait_ge(made, c + 1)
                    sp.dma_start(table[bass.ds(c * NC * P, NC * P), :].rearrange("(b p) d -> p b d", p=P),
                                 rows[:, bass.ds(c * NC, NC), :]).then_inc(stored, 16)

            def park(r):
                with sp.Fori(0, RG) as t:
                    for j in range(RG):
                        sp.wait_ge(gathered[j], t * (16 * GT) + 16 * GT * (2 * r * RTN + 1))
                        sp.dma_start(parked_d[bass.ds(t * RG + j, 1), :, :].rearrange("a p n -> (a p) n"),
                                     ring[:, j, :, :]).then_inc(parked[j], 16)
                for j in range(RG):
                    sp.wait_ge(parked[j], 16 * RG * (r + 1))

            def reload(p, t, j):
                sp.wait_ge(s("summed"), t * UG + (summed_by(p, 1) + 2 * (j - last_use(BACK, j))))
                sp.dma_start(ring[:, RG + BACK[j], :, :], parked_d[bass.ds(t * RG + j, 1), :, :].rearrange("a p n -> (a p) n")
                             ).then_inc(reloaded[j], 16)

            park(0)
            with sp.Fori(0, IT) as t:
                for j in range(RG):
                    reload(0, t, j)

            def rh_rows(q, n=GT):
                return edge_attr[bass.ds(q * GE, n * P), :].rearrange("(t p) d -> p t d", p=P)

            def load_last_rh(tile, loaded, tails):
                sp.dma_start(tile[0:FR, FT - (G - 1) * GT, :], edge_attr[FT * P:E, :]).then_inc(s("tail_loaded"), 16)
                sp.wait_ge(s("tail_loaded"), 16 * tails)
                sp.dma_start(tile[:, 0:FT - (G - 1) * GT, :], rh_rows(G - 1, FT - (G - 1) * GT)).then_inc(loaded, 16)

            store_chunks(h1_d, s("h1_made"), s("h1_stored"))
            for j in range(2):
                sp.wait_ge(lo_loaded[j], 16 * (G // 2 + 1))
            for j in range(2):
                sp.dma_start(rh[:, j], rh_rows(j)).then_inc(rh_loaded[j], 16)
            with sp.Fori(1, G // 2 - 1) as i:
                for j in range(2):
                    sp.wait_ge(s("rh_dotted"), i * 2 + (j - 1))
                    sp.dma_start(rh[:, j], rh_rows(i * 2 + j)).then_inc(rh_loaded[j], 16)
            sp.wait_ge(s("rh_dotted"), G - 3)
            sp.dma_start(rh[:, 0], rh_rows(G - 2)).then_inc(rh_loaded[0], 16)
            sp.wait_ge(s("rh_dotted"), G - 2)
            load_last_rh(rh[:, 1], rh_loaded[1], 1)
            store_chunks(x2_d, s("x2_made"), s("x2_stored"), xsb)
            park(1)
            sp.wait_ge(s("selected"), 2 * G + 1)
            for j in range(2):
                sp.wait_ge(lo_loaded[j], 16 * (G + 2))
                sp.wait_ge(rank_loaded[j], 16 * (G // 2 + 1))

            def load_pair(t, j, last=False):
                reload(2, t, j)
                for h in range(2):
                    n = 2 * j + h
                    q, _ = group(2, t, n)
                    sp.wait_ge(s("summed"), t * UG + (summed_by(2, 1) + n - last_use(RHS, n)))
                    if last and h:
                        load_last_rh(rhv[RHS[n]], rh2_loaded[n], 2)
                    else:
                        sp.dma_start(rhv[RHS[n]], rh_rows(q)).then_inc(rh2_loaded[n], 16)

            with sp.Fori(0, IT - 1) as t:
                for j in range(RG):
                    load_pair(t, j)
            for j in range(RG):
                load_pair(IT - 1, j, j == RG - 1)
            with sp.Fori(0, NCH - 1) as c:
                sp.wait_ge(s("out_made"), c + 2)
                sp.dma_start(out[bass.ds(c * NC * P, NC * P), :].rearrange("(b p) d -> p b d", p=P),
                             xsb[:, bass.ds(c * NC, NC), :]).then_inc(s("out_stored"), 16)
            sp.wait_ge(s("out_made"), NCH + 1)
            sp.dma_start(out[(NCH - 1) * NC * P:(NB - 1) * P, :].rearrange("(b p) d -> p b d", p=P),
                         xsb[:, (NCH - 1) * NC:NB - 1, :]).then_inc(s("out_stored"), 16)
            sp.dma_start(out[(NB - 1) * P:N, :], xsb[0:NLAST, NB - 1, :]).then_inc(s("out_stored"), 16)
            sp.wait_ge(s("out_stored"), 16 * (NCH + 1))

        @block.gpsimd
        def _(pool):
            nc.gpsimd.memset(srcR[:, EB - 1, :], 0).then_inc(s("pads_set"), 1)
            nc.gpsimd.memset(dstR[:, EB - 1, :], int(FAR)).then_inc(s("pads_set"), 1)
            nc.gpsimd.memset(ewR[:, EB - 1, :], 0.0).then_inc(s("pads_set"), 1)
            nc.gpsimd.memset(xsb[:, NB - 1, :], 0.0).then_inc(s("pads_set"), 1)
            nc.gpsimd.memset(dprevL[:, 0:LW], -1).then_inc(s("pads_set"), 1)
            nc.gpsimd.memset(dnextL[:, 0:LW], -1).then_inc(s("pads_set"), 1)
            nc.gpsimd.iota(iota_i[:, :], [[1, P]], base=0, channel_multiplier=0).then_inc(s("iota_made"), 1)
            nc.gpsimd.iota(pidx_i[:, :], [[1, 1]], base=0, channel_multiplier=1).then_inc(s("iota_made"), 1)
            nc.gpsimd.memset(acc[:, 0, NB * P:NA], 0.0).then_inc(s("tails_set"), 1)
            nc.gpsimd.memset(x2T[:, :], 0.0).then_inc(s("tails_set"), 1)
            nc.gpsimd.memset(ones_h[:, :], 1.0).then_inc(s("tails_set"), 1)
            nc.gpsimd.memset(ones3[:, :], 1.0).then_inc(s("tails_set"), 1)
            nc.gpsimd.memset(epsc[:, :], EPS).then_inc(s("tails_set"), 1)

            def turn(p, table, t, half, free):
                first = p == 0 and isinstance(t, int)
                pool.wait_ge(s("staged"), t + (p * RTN + 1))
                for j in range(RG):
                    free(j)
                    pool.sem_inc(s("pool_passed"))
                    for k in range(GT):
                        c = j * GT + k
                        pool.indirect_dma_start(
                            ring[:, j, k, :], None, table[:, :],
                            bass.IndirectOffsetOnAxis(ap=stage[:, half, c:c + 1], axis=0)).then_inc(gathered[j], 16)
                    if j == RG // 2:
                        for m in range(RG):
                            if not (isinstance(t, int) and t + p == 0):
                                pool.wait_ge(gathered[m], t * (16 * GT) + 16 * GT * p * RTN)
                        pool.sem_inc(s("pool_passed"))
                        nc.gpsimd.tensor_copy(stage[:, 1 - half, :], srcC[:, bass.ds(t * RT + RT, RT)]).then_inc(s("staged"), 1)

            def parked_pass(p, table):
                r = p // 2
                turn(p, table, 0, 0, lambda j: None)
                with pool.Fori(0, RG // 2) as i:
                    for h in range(2):
                        turn(p, table, i * 2 + (1 + h), 1 - h, lambda j: pool.wait_ge(parked[j], i * 32 + 16 * (r * RG + 1 + h)))
                turn(p, table, RG, 1, lambda j: pool.wait_ge(parked[j], 16 * RG * (r + 1)))
                with pool.Fori(0, RG // 2) as i:
                    for h in range(2):
                        turn(p, table, i * 2 + (RG + 1 + h), h,
                             lambda j: pool.wait_ge(s("summed"), i * (2 * UG) + (summed_by(p, 2 * j + 2) + h * UG)))

            pool.wait_ge(s("src_cols"), 1)
            nc.gpsimd.tensor_copy(stage[:, 0, :], srcC[:, 0:RT]).then_inc(s("staged"), 1)
            parked_pass(0, x)
            pool.wait_ge(s("h1_stored"), 16 * NCH)
            with pool.Fori(0, RTN // 2) as i:
                for h in range(2):
                    turn(1, h1_d, i * 2 + h, h, lambda j: pool.wait_ge(s("summed"), i * UG + (summed_by(1, j + 1) + (h - 1) * RG)))
            nc.gpsimd.memset(s1P, 0.0).then_inc(s("s1_cleared"), 1)
            pool.wait_ge(s("x2_stored"), 16 * NCH)
            parked_pass(2, x2_d)

        @block.tensor
        def _(pe):
            nbatch = 0
            pe.wait_ge(s("ident_made"), 1)

            def rows_to_cols(tile, ready, count):
                nonlocal nbatch
                pe.wait_ge(ready, count)
                for h in range(2):
                    if nbatch >= 2:
                        pe.wait_ge(s("cols_copied"), nbatch - 1)
                    n = min(4, EB - 4 * h)
                    for b in range(n):
                        last = nc.tensor.transpose(ps[nbatch % 2][:, b * P:(b + 1) * P], tile[:, 4 * h + b, :], ident[:, :])
                    last.then_inc(s("cols_ready"), 1)
                    nbatch += 1

            rows_to_cols(rowF[:, 1], s("rowF_made"), 1)
            rows_to_cols(rowF[:, 2], s("rowF_made"), 2)
            rows_to_cols(rowF[:, 0], s("rowF_made"), 3)
            pe.wait_ge(s("dmin_made"), 1)
            nc.tensor.transpose(ps[2][0:EB, 0:P], dmin[:, :], ident[:, :]).then_inc(s("dmin_turned"), 1)
            rows_to_cols(ewR, s("ew_loaded"), 16 * (EB + 1))
            pe.wait_ge(s("weights_loaded"), 16 * 8)
            nc.tensor.transpose(ps[3][:, 0:P], fcw[:, :], ident[:, :])
            nc.tensor.transpose(ps[3][:, P:2 * P], fcrw[:, :], ident[:, :])
            nc.tensor.matmul(ps[3][:, 2 * P:3 * P], fcw[:, :], lw[:, :], start=True, stop=True)
            nc.tensor.transpose(ps[3][:, 3 * P:3 * P + 3], aw3[:, :], ident[0:3, 0:3]).then_inc(s("wprod"), 1)
            pe.wait_ge(s("awT_copied"), 2)
            nc.tensor.matmul(ps[4][:, 0:2], fcw[:, :], awT[:, 0:2], start=True, stop=True)
            nc.tensor.matmul(ps[4][:, P:2 * P], a2B[:, :], fcrw[:, :], start=True, stop=True).then_inc(s("wprod"), 1)
            pe.wait_ge(s("rank_made"), 1)
            for h in range(2):
                pe.wait_ge(s("cols_copied"), nbatch - 1)
                n = min(4, EB - 4 * h)
                for b in range(n):
                    last = nc.tensor.transpose(ps[nbatch % 2][:, b * P:(b + 1) * P],
                                               rankC[:, (4 * h + b) * P:(4 * h + b + 1) * P], ident[:, :])
                last.then_inc(s("cols_ready"), 1)
                nbatch += 1

            with pe.Fori(0, G // 2) as i:
                for j in range(2):
                    pe.wait_ge(s("deg_onehot"), i * 2 + (j + 1))
                    for k in range(GT):
                        last = nc.tensor.matmul(ps[5 + j][0:3, 0:W], ewS[:, j, k, :], SH[:, j, k, 0:W],
                                                start=(k == 0), stop=(k == GT - 1))
                    last.then_inc(s("deg_summed"), 1)
            pe.wait_ge(s("deg_state"), G + 1)
            for b in range(NB):
                last = nc.tensor.matmul(ps[7][:, b:b + 1], deg3[0:3, b * P:(b + 1) * P], ones3[0:3, 0:1],
                                        start=True, stop=True)
            last.then_inc(s("deg_cols"), 1)
            for c in range(NCH):
                pe.wait_ge(s("x1_made"), c + 1)
                for b in range(NC):
                    if b % 4 == 0:
                        pe.wait_ge(s("x1_evac"), c * 2 + (b // 4 + 1))
                    last = nc.tensor.transpose(ps[b // 4][:, (b % 4) * P:(b % 4 + 1) * P],
                                               rows[:, c * NC + b, :], ident[:, :])
                    if b in (3, NC - 1):
                        last.then_inc(s("x1_turned"), 1)

            def lookups(r):
                with pe.Fori(0, G // 2) as i:
                    for j in range(2):
                        pe.wait_ge(s("onehot_built"), i * 2 + (j + 1 + r * (G + 1)))
                        for k in range(GT):
                            for part in range(3):
                                last = nc.tensor.matmul(ps[4 + j][:, 64 * k:64 * k + NB], ohL[:, j, k * P:(k + 1) * P], tab[:, part, :],
                                                        start=(part == 0), stop=(part == 2))
                        for k in range(GT if r else 0):
                            for part in range(3):
                                last = nc.tensor.matmul(ps[2 + j][:, k:k + 1], ohR[:, j, k * P:(k + 1) * P],
                                                        s1w[:, part, bass.ds(i * 2 + j, 1)], start=(part == 0), stop=(part == 2))
                        last.then_inc(s("looked_up"), 1)

            pe.sem_inc(s("summed"), CREDIT)
            pe.wait_ge(s("tables_split"), 1)
            lookups(0)

            def sum_pass(p):
                with pe.Fori(0, IT) as it:
                    for j in range(UG):
                        _, slot = group(p, 0, j)
                        if p == 1:
                            pe.wait_ge(gathered[slot], it * (2 * 16 * GT) + 16 * GT * (RTN + 1 + j // RG))
                        elif j % 2:
                            pe.wait_ge(gathered[slot], it * (16 * GT) + 16 * GT * (p * RTN + RG + 1))
                        else:
                            pe.wait_ge(reloaded[j // 2], it * 16 + 16 * (p // 2 * IT + 1))
                        pe.wait_ge(s("S_built"), it * UG + (p * (G + 1) + j + 1))
                        for k in range(GT):
                            last = nc.tensor.matmul(ps[2 + j % 2][:, 0:W], ring[:, slot, k, :], S[:, j % 2, k, :],
                                                    start=(k == 0), stop=(k == GT - 1))
                        if p == 2:
                            pe.wait_ge(rh2_loaded[j], it * 16 + 16)
                            for k in range(GT):
                                last = nc.tensor.matmul(ps[2 + j % 2][:, W:2 * W], rhv[RHS[j]][:, k, :], S[:, j % 2, k, :],
                                                        start=(k == 0), stop=(k == GT - 1))
                        last.then_inc(s("summed"), 1)

            sum_pass(0)
            def layer(weight, ready, count, made, evac, turned, psA, rows=rows):
                pe.wait_ge(ready, count)
                for c in range(NCH):
                    for b in range(NC):
                        pe.wait_ge(psA[0], c * NC + (b + 1))
                        nc.tensor.matmul(ps[4 + b % 4][:, 0:D], acc[:, 0, (c * NC + b) * P:(c * NC + b + 1) * P], weight[:, :],
                                         start=True, stop=True).then_inc(psA[1], 1)
                    pe.wait_ge(made, c + 1)
                    for b in range(NC):
                        if b % 4 == 0:
                            pe.wait_ge(evac, c * 2 + (b // 4 + 1))
                        last = nc.tensor.transpose(ps[b // 4][:, (b % 4) * P:(b % 4 + 1) * P],
                                                   rows[:, c * NC + b, :], ident[:, :])
                        if b in (3, NC - 1):
                            last.then_inc(turned, 1)

            layer(w1, s("acc_added"), G + 1, s("h1_made"), s("h1_evac"), s("h1_turned"), (s("l1_free"), s("l1_prod")))
            sum_pass(1)
            layer(w2, s("acc_added"), 2 * G + 2, s("x2_made"), s("x2_evac"), s("x2_turned"), (s("l2_free"), s("l2_prod")), xsb)
            pe.wait_ge(s("x2_evac"), 2 * NCH + 2)
            for b in range(NB):
                last = nc.tensor.matmul(ps[6][:, 2 * b:2 * b + 2], x2T[:, b * P:(b + 1) * P], v01[:, :], start=True, stop=True)
            last.then_inc(s("scores"), 1)
            pe.wait_ge(s("tables_split"), 2)
            for part in range(3):
                last = nc.tensor.transpose(ps[1][0:NB, part * 64:(part + 1) * 64].bitcast(BF16), s1p[:, part, :], ident_h[:, :])
            last.then_inc(s("s1_turned"), 1)
            pe.wait_ge(s("s1_loaded"), 16)
            with pe.Fori(0, G // 2) as i:
                for j in range(2):
                    b = pe.value_load(base_row[0:1, bass.ds(i * 2 + j, 1)], min_val=0, max_val=N - 1)
                    last = nc.tensor.matmul(ps[7][:, bass.ds(i * 2 + j, 1)], s1P[:, bass.ds(b, W)], ones_h[:, :],
                                            start=True, stop=True)
                last.then_inc(s("windows"), 1)
            pe.wait_ge(s("tables_split"), 4)
            lookups(1)
            pe.wait_ge(s("e_cols"), 1)
            for h in range(2):
                n = min(4, EB - 4 * h)
                for b in range(n):
                    last = nc.tensor.transpose(ps[h][:, b * P:(b + 1) * P], eC[:, (4 * h + b) * P:(4 * h + b + 1) * P], ident[:, :])
                last.then_inc(s("e_turned"), 1)
            for n in range(4):
                pe.wait_ge(s("ends_made"), n + 1)
                nc.tensor.transpose(ps[6][0:1, 0:LP], lend[0:LP, 0:1], ident[0:LP, 0:LP])
                nc.tensor.transpose(ps[6][0:1, P:P + LP], lend[0:LP, 1:2], ident[0:LP, 0:LP]).then_inc(s("ends_turned"), 1)
                pe.wait_ge(s("carry_made"), n + 1)
                off = 2 if n % 2 else 0
                nc.tensor.transpose(ps[7][0:LP, 0:1], lcar[0:1, off:off + LP], ident[0:1, 0:1]).then_inc(s("carry_turned"), 1)
            pe.wait_ge(s("alpha_loaded"), 16 * (EB + 1))
            for h in range(2):
                n = min(4, EB - 4 * h)
                for b in range(n):
                    last = nc.tensor.transpose(ps[h][:, b * P:(b + 1) * P], rowF[:, 0, 4 * h + b, :], ident[:, :])
                last.then_inc(s("alpha_turned"), 1)
            sum_pass(2)
            pe.wait_ge(s("acc_added"), 3 * G + 3)
            for c in range(NCH):
                for b in range(NC):
                    pe.wait_ge(s("fin_free"), c * NC + (b + 1))
                    blk = slice((c * NC + b) * P, (c * NC + b + 1) * P)
                    nc.tensor.matmul(ps[4 + b % 4][:, 0:D], acc[:, 0, blk], fcwT[:, :], start=True, stop=False)
                    nc.tensor.matmul(ps[4 + b % 4][:, 0:D], acc[:, 1, blk], fcrwT[:, :], start=False, stop=False)
                    nc.tensor.matmul(ps[4 + b % 4][:, 0:D], x2T[:, blk], wz[:, :], start=False, stop=True
                                     ).then_inc(s("fin_prod"), 1)

        @block.scalar
        def _(act):
            act.wait_ge(s("deg_clamped"), 1)
            nc.scalar.activation(dtmp[:, 0, :], dtmp[:, 0, :], ACT.Sqrt).then_inc(s("deg_root"), 1)

            def evacuate(turned, count, evac, dest, col0, ready=None):
                with act.Fori(0, NCH) as c:
                    for h in range(2):
                        n = 4 if h == 0 else NC - 4
                        act.wait_ge(turned, c * 2 + (h + 1 + count))
                        act.sem_inc(s("act_passed"))
                        nc.scalar.copy(dest[:, bass.ds(c * (NC * P) + h * 4 * P, n * P)], ps[h][:, 0:n * P]
                                       ).then_inc(evac, 1)

            evacuate(s("x1_turned"), 0, s("x1_evac"), acc[:, 0, :], 0)

            def load_lo(r):
                def one(q, j):
                    for dram, tile, loaded in ((lo_d, loB, lo_loaded[j]), (rank_d, rankB, rank_loaded[j]))[:1 + r]:
                        act.dma_start(tile[:, j, :], dram[bass.ds(q * GE, GE)].rearrange("(a n) -> a n", a=1)
                                      .broadcast_to([P, GE])).then_inc(loaded, 16)
                for j in range(2):
                    one(j, j)
                with act.Fori(1, G // 2 + 1) as i:
                    for j in range(2):
                        act.wait_ge(s("onehot_built"), i * 2 + (j - 1 + r * (G + 1)))
                        one(i * 2 + j, j)

            act.wait_ge(s("lo_stored"), 32)
            load_lo(0)
            evacuate(s("h1_turned"), 0, s("h1_evac"), acc[:, 0, :], 0)
            with act.Fori(0, NCH) as c:
                for b in range(NC):
                    act.wait_ge(s("l2_free"), c * NC + (b + 4))
                    nc.scalar.activation(u[:, b, :], u[:, b, :], ACT.Sigmoid).then_inc(s("l2_sigm"), 1)
                act.wait_ge(s("l2_stats"), c + 1)
                nc.scalar.activation(sd[:, :], mv[:, :, 1], ACT.Sqrt, bias=epsc[:, 0:1]).then_inc(s("l2_root"), 1)
                for h in range(2):
                    n = 4 if h == 0 else NC - 4
                    act.wait_ge(s("x2_turned"), c * 2 + (h + 1))
                    act.sem_inc(s("act_passed"))
                    nc.scalar.copy(x2T[:, bass.ds(c * (NC * P) + h * 4 * P, n * P)], ps[h][:, 0:n * P]
                                   ).then_inc(s("x2_evac"), 1)
            act.wait_ge(s("s1_rows"), 1)
            act.dma_start(s1_d[:, :].rearrange("k (a p) -> a k p", p=P), s1rows[:, :, :]).then_inc(s("s1_stored"), 16)
            act.wait_ge(s("s1_stored"), 16)
            act.wait_ge(s("s1_cleared"), 1)
            act.dma_start(s1P[0:3, 0:NB * P], s1_d[:, :]).then_inc(s("s1_loaded"), 16)
            load_lo(1)
            act.wait_ge(s("e_rows"), 2)
            act.dma_start(e_d.rearrange("(b t p) -> t b p", t=P, p=P), rowF[:, 0, :, :]).then_inc(s("e_stored"), 16)
            act.wait_ge(s("e_stored"), 16)
            act.dma_start(eL, e_d[0:E].rearrange("(p j) -> p j", p=LP)).then_inc(s("e_loaded"), 16)
            act.wait_ge(s("e_shifted"), 1)
            nc.scalar.activation(eL, eL, ACT.Exp).then_inc(s("e_exp"), 1)
            act.wait_ge(s("alpha_made"), 1)
            act.dma_start(al_d.rearrange("(p j) -> p j", p=LP), mL).then_inc(s("alpha_stored"), 16)
            act.wait_ge(s("alpha_stored"), 16)
            for b in range(EB - 1):
                act.dma_start(rowF[:, 0, b, :], erows(al_d, b * P, P)).then_inc(s("alpha_loaded"), 16)
            act.dma_start(rowF[0:REST, 0, EB - 1, :], erows(al_d, (EB - 1) * P, REST)).then_inc(s("alpha_loaded"), 16)
            act.dma_start(rowF[REST:REST + 1, 0, EB - 1, 0:FR], al_d[FT * P:E].rearrange("(a n) -> a n", a=1)
                         ).then_inc(s("alpha_loaded"), 16)
            with act.Fori(0, NCH) as c:
                act.wait_ge(s("fin_stats"), c + 1)
                nc.scalar.activation(sd[:, :], mv[:, :, 1], ACT.Sqrt, bias=epsc[:, 0:1]).then_inc(s("fin_root"), 1)

        @block.vector
        def _(dve):
            v = nc.vector
            steps = [0]

            def link(ins):
                steps[0] += 1
                ins.then_inc(s("dve_step"), 1)
                dve.wait_ge(s("dve_step"), steps[0])

            dve.wait_ge(s("iota_made"), 2)
            link(v.tensor_copy(pidx[:, :], pidx_i[:, :]))
            v.tensor_copy(iota_h[:, :], iota_i[:, :])
            link(v.tensor_copy(iota[:, :], iota_i[:, :]))
            v.tensor_scalar(ident_h[:, :], iota[:, :], pidx[:, 0:1], None, ALU.is_equal)
            v.tensor_scalar(ident[:, :], iota[:, :], pidx[:, 0:1], None, ALU.is_equal).then_inc(s("ident_made"), 1)
            dve.wait_ge(s("src_loaded"), 16 * (EB + 1))
            v.tensor_copy(rowF[:, 1], srcR).then_inc(s("rowF_made"), 1)
            v.tensor_scalar(loI, srcR, P - 1, None, ALU.bitwise_and).then_inc(s("lo_split"), 1)
            ncol = [0]

            def cols_from(dest):
                for h in range(2):
                    n = min(4, EB - 4 * h) * P
                    ncol[0] += 1
                    dve.wait_ge(s("cols_ready"), ncol[0])
                    last = v.tensor_copy(dest[:, 4 * P * h:4 * P * h + n], ps[(ncol[0] - 1) % 2][:, 0:n])
                    last.then_inc(s("cols_copied"), 1)

            cols_from(srcC)
            dve.wait_ge(s("cols_copied"), ncol[0])
            v.tensor_copy(srcC[:, T:T + RT], srcC[:, 0:RT]).then_inc(s("src_cols"), 1)
            dve.wait_ge(s("lo_split"), 1)
            v.tensor_copy(loH[:, :, :], loI).then_inc(s("lo_made"), 1)
            dve.wait_ge(s("lo_made"), 1)
            link(v.tensor_scalar(loI, srcR, 7, None, ALU.arith_shift_right))
            v.tensor_copy(rowF[:, 2], loI).then_inc(s("rowF_made"), 1)
            dve.wait_ge(s("dst_loaded"), 16 * (EB + 1))
            v.tensor_copy(rowF[:, 0], dstR).then_inc(s("rowF_made"), 1)
            dve.wait_ge(s("rowF_made"), 3)
            v.tensor_reduce(dmin[:, :], rowF[:, 0], AX.X, ALU.min).then_inc(s("dmin_made"), 1)
            cols_from(hiC)
            cols_from(rankC)
            dve.wait_ge(s("dmin_turned"), 1)
            link(v.tensor_reduce(base7[:, :], ps[2][0:EB, 0:P].rearrange("a (g t) -> a g t", t=GT), AX.X, ALU.min))
            v.tensor_copy(base7i[:, :], base7[:, :]).then_inc(s("base_made"), 2)
            cols_from(ewC)
            dve.wait_ge(s("cols_copied"), ncol[0])
            split_tmp = t2C[:, :]
            link(v.tensor_copy(ewP[:, :, 0], ewC[:, :]))
            link(v.tensor_tensor(split_tmp, ewC[:, :], ewP[:, :, 0], ALU.subtract))
            link(v.tensor_copy(ewP[:, :, 1], split_tmp))
            link(v.tensor_tensor(split_tmp, split_tmp, ewP[:, :, 1], ALU.subtract))
            link(v.tensor_copy(ewP[:, :, 2], split_tmp))
            dve.wait_ge(s("lin_loaded"), 16 * 5)
            v.tensor_tensor(penN[:, :], dL, dnextL, ALU.is_equal)
            link(v.tensor_tensor(sameL[:, :], dL, dprevL, ALU.is_equal))
            link(v.tensor_scalar(penL[:, :], sameL[:, :], -1.0, BIG, ALU.add, ALU.mult))
            link(v.tensor_scalar(penN[:, :], penN[:, :], -1.0, BIG, ALU.add, ALU.mult))
            dve.wait_ge(s("base_loaded"), 32)
            rk = rankC[:, :].rearrange("p (g t) -> p g t", t=GT)
            v.tensor_tensor(rk, rk, baseB[:, :].unsqueeze(2).broadcast_to([P, EB * 16, GT]), ALU.subtract
                            ).then_inc(s("rank_made"), 1)
            dve.wait_ge(s("wprod"), 1)
            v.tensor_copy(fcwT[:, :], ps[3][:, 0:P])
            v.tensor_copy(fcrwT[:, :], ps[3][:, P:2 * P])
            v.tensor_copy(wz[:, :], ps[3][:, 2 * P:3 * P])
            v.tensor_copy(awT[:, :], ps[3][:, 3 * P:3 * P + 3]).then_inc(s("awT_copied"), 1)
            dve.wait_ge(s("awT_copied"), 1)
            v.tensor_copy(a2B[:, :], awT[:, 2:3].broadcast_to([P, P])).then_inc(s("awT_copied"), 1)
            dve.wait_ge(s("wprod"), 2)
            v.tensor_copy(v01[:, :], ps[4][:, 0:2])
            v.tensor_copy(v2B[:, :], ps[4][:, P:2 * P]).then_inc(s("v_made"), 1)
            dve.wait_ge(s("lo_stored"), 16)
            for h in range(2):
                ncol[0] += 1
                n = min(4, EB - 4 * h)
                dve.wait_ge(s("cols_ready"), ncol[0])
                v.tensor_copy(loH[:, 4 * h:4 * h + n, :], ps[(ncol[0] - 1) % 2][:, 0:n * P].rearrange("p (b t) -> p b t", t=P)
                              ).then_inc(s("rank_rows"), 1)

            dve.wait_ge(s("rank_made"), 1)
            dve.wait_ge(s("tails_set"), 5)

            def deg_onehot(q, slot):
                v.tensor_copy(ewS[:, slot, :, :], ewP[:, ecols(q), :])
                for k in range(GT):
                    last = v.tensor_scalar(SH[:, slot, k, 0:W], iota_h[:, :], rankC[:, bass.ds(q * GT + k, 1)], None, ALU.is_equal)
                last.then_inc(s("deg_onehot"), 1)

            deg_onehot(0, 0)
            dve.sem_inc(s("deg_state"), 1)
            with dve.Fori(0, G // 2) as i:
                for j in range(2):
                    deg_onehot(i * 2 + (j + 1), (j + 1) % 2)
                    b = dve.value_load(base_row[0:1, bass.ds(i * 2 + j, 1)], min_val=0, max_val=N - 1)
                    win = deg3[:, bass.ds(b, W)]
                    dve.wait_ge(s("deg_state"), i * 2 + (j + 1))
                    dve.wait_ge(s("deg_summed"), i * 2 + (j + 1))
                    ins = v.tensor_tensor(win, ps[5 + j][0:3, 0:W], win, ALU.add)
                    ins.then_inc(s("deg_state"), 1)
            dve.wait_ge(s("deg_cols"), 1)
            link(v.tensor_scalar(dinv[:, :], ps[7][:, 0:NB], 1.0, None, ALU.add))
            v.tensor_scalar(dtmp[:, 0, :], dinv[:, :], 1e-30, None, ALU.max).then_inc(s("deg_clamped"), 1)
            link(v.tensor_scalar(dtmp[:, 1, :], dinv[:, :], 0.0, None, ALU.is_gt))
            dve.wait_ge(s("deg_root"), 1)
            link(v.reciprocal(dtmp[:, 0, :], dtmp[:, 0, :]))
            link(v.tensor_tensor(dinv[:, :], dtmp[:, 0, :], dtmp[:, 1, :], ALU.mult))
            dve.wait_ge(s("x_loaded"), 16 * 7)
            dve.sem_inc(s("x1_evac"), 2)
            with dve.Fori(0, NCH) as c:
                for b in range(NC):
                    last = v.tensor_scalar(rows[:, c * NC + b, :], xsb[:, c * NC + b, :],
                                           dinv[:, bass.ds(c * NC + b, 1)], None, ALU.mult)
                last.then_inc(s("x1_made"), 1)

            def split3(parts, full, tmp):
                link(v.tensor_copy(parts[:, 0, :], full))
                link(v.tensor_tensor(tmp, full, parts[:, 0, :], ALU.subtract))
                link(v.tensor_copy(parts[:, 1, :], tmp))
                link(v.tensor_tensor(tmp, tmp, parts[:, 1, :], ALU.subtract))
                v.tensor_copy(parts[:, 2, :], tmp).then_inc(s("tables_split"), 1)

            def onehots(r, q, i, j):
                dve.wait_ge(lo_loaded[j], i * 16 + 16 * (r * (G // 2 + 1) + 1))
                last = v.tensor_scalar(ohL[:, j, :], loB[:, j, :], pidx[:, 0:1], None, ALU.is_equal)
                if r:
                    dve.wait_ge(rank_loaded[j], i * 16 + 16)
                    last = v.tensor_scalar(ohR[:, j, :], rankB[:, j, :], pidx[:, 0:1], None, ALU.is_equal)
                last.then_inc(s("onehot_built"), 1)

            def lookups(r, dest):
                onehots(r, 0, 0, 0)
                with dve.Fori(0, G // 2) as i:
                    for j in range(2):
                        q = i * 2 + j
                        onehots(r, q + 1, i + j, (j + 1) % 2)
                        dve.wait_ge(s("looked_up"), i * 2 + (j + 1 + r * G))
                        if r:
                            v.tensor_tensor(eC[:, ecols(q)], ps[2 + j][:, 0:GT], t2C[:, ecols(q)], ALU.add)
                        dve.wait_ge(s("selected"), i * 2 + (j + 1 + r * G))
                        for k in range(GT):
                            col = bass.ds(q * GT + k, 1)
                            last = v.scalar_tensor_tensor(prod[:, k, :], iota[:, 0:NB], hiC[:, col], ps[4 + j][:, 64 * k:64 * k + NB],
                                                          ALU.is_equal, ALU.mult, accum_out=dest[:, col])
                        last.then_inc(s("selected"), 1)

            dve.wait_ge(s("x1_evac"), 2 * NCH + 2)
            split3(tab, dinv[:, :], dtmp[:, 1, :])
            dve.sem_inc(s("selected"), 1)
            lookups(0, t2C)
            dve.wait_ge(s("selected"), G + 1)
            link(v.tensor_tensor(t2C[:, 0:T], t2C[:, 0:T], ewC[:, 0:T], ALU.mult))
            def build_S(q, slot, wcols):
                for k in range(GT):
                    col = bass.ds(q * GT + k, 1)
                    last = v.tensor_scalar(S[:, slot, k, :], iota[:, :], rankC[:, col], wcols[:, col], ALU.is_equal, ALU.mult)
                last.then_inc(s("S_built"), 1)

            def edge_pass(p, wcols, extra=None):
                naccs = 2 if p == 2 else 1
                build_S(0, 0, wcols)
                with dve.Fori(0, IT) as it:
                    for j in range(UG):
                        q, _ = group(p, it, j)
                        build_S(group(p, it, j + 1)[0], (j + 1) % 2, wcols)
                        if extra:
                            extra(q, it, j)
                        b = dve.value_load(base_row[0:1, bass.ds(q, 1)], min_val=0, max_val=N - 1)
                        win = acc[:, 0:naccs, bass.ds(b, W)]
                        dve.wait_ge(s("acc_added"), it * UG + (p * (G + 1) + j + 1))
                        dve.wait_ge(s("summed"), it * UG + summed_by(p, j + 1))
                        v.tensor_tensor(win, ps[2 + j % 2][:, 0:naccs * W].rearrange("p (a w) -> p a w", a=naccs), win, ALU.add
                                        ).then_inc(s("acc_added"), 1)

            dve.sem_inc(s("acc_added"), 1)
            edge_pass(0, t2C)
            dve.wait_ge(s("acc_added"), G + 1)
            dve.sem_inc(s("l1_free"), 3)
            dve.sem_inc(s("h1_evac"), 2)
            with dve.Fori(0, NCH) as c:
                for b in range(NC):
                    col = bass.ds(c * NC + b, 1)
                    dve.wait_ge(s("l1_prod"), c * NC + (b + 1))
                    v.scalar_tensor_tensor(u[:, b, :], ps[4 + b % 4][:, 0:D], dinv[:, col], b1B[:, :], ALU.mult, ALU.add
                                           ).then_inc(s("l1_free"), 1)
                for b in range(NC):
                    dve.wait_ge(s("l1_free"), c * NC + (b + 4))
                    last = v.tensor_scalar(rows[:, c * NC + b, :], u[:, b, :], 0.0, dinv[:, bass.ds(c * NC + b, 1)], ALU.max, ALU.mult)
                last.then_inc(s("h1_made"), 1)

            def dots(q, it, j):
                dve.wait_ge(rh_loaded[j % 2], it * (16 * UG // 2) + (16 * (j // 2 + 1)))
                dve.sem_inc(s("dve_passed"))
                for k in range(GT):
                    last = v.scalar_tensor_tensor(rh[:, j % 2, k, :], rh[:, j % 2, k, :], 1.0, v2B[:, :], ALU.mult, ALU.mult,
                                                  accum_out=t2C[:, bass.ds(q * GT + k, 1)])
                last.then_inc(s("rh_dotted"), 1)

            dve.wait_ge(s("h1_evac"), 2 * NCH + 2)
            dve.sem_inc(s("acc_added"), 1)
            edge_pass(1, ewC, dots)

            dve.wait_ge(s("acc_added"), 2 * G + 2)
            dve.sem_inc(s("l2_free"), 3)
            dve.sem_inc(s("x2_evac"), 2)
            dve.wait_ge(s("h1_stored"), 16 * NCH)
            with dve.Fori(0, NCH) as c:
                for b in range(NC):
                    col = bass.ds(c * NC + b, 1)
                    dve.wait_ge(s("l2_prod"), c * NC + (b + 1))
                    v.scalar_tensor_tensor(u[:, b, :], ps[4 + b % 4][:, 0:D], dinv[:, col], b2B[:, :], ALU.mult, ALU.add
                                           ).then_inc(s("l2_free"), 1)
                for b in range(NC):
                    dve.wait_ge(s("l2_sigm"), c * NC + (b + 1))
                    v.tensor_tensor(u[:, b, :], u[:, b, :], xsb[:, c * NC + b, :], ALU.add).then_inc(s("l2_res"), 1)
                for b in range(NC):
                    dve.wait_ge(s("l2_res"), c * NC + (b + 1))
                    v.bn_stats(bst[:, b, :], u[:, b, :]).then_inc(s("l2_bn"), 1)
                dve.wait_ge(s("l2_bn"), c * NC + NC)
                dve.sem_inc(s("dve_passed"))
                for b in range(NC):
                    last = v.bn_aggr(mv[:, b, :], bst[:, b, :])
                last.then_inc(s("l2_stats"), 1)
                dve.wait_ge(s("l2_root"), c + 1)
                v.reciprocal(rs[:, :], sd[:, :]).then_inc(s("l2_rs"), 1)
                dve.wait_ge(s("l2_rs"), c + 1)
                for b in range(NC):
                    last = v.tensor_scalar(xsb[:, c * NC + b, :], u[:, b, :], mv[:, b, 0:1], rs[:, b:b + 1], ALU.subtract, ALU.mult)
                last.then_inc(s("x2_made"), 1)

            dve.wait_ge(s("scores"), 1)
            score = ps[6][:, 0:2 * NB].rearrange("p (b k) -> p b k", k=2)
            v.tensor_copy(tabf[:, :], score[:, :, 0])
            link(v.tensor_copy(s1f[:, 0:NB], score[:, :, 1]))
            split3(s1p, s1f[:, 0:NB], dtmp[:, 0, :])
            split3(tab, tabf[:, :], dtmp[:, 1, :])
            dve.wait_ge(s("s1_turned"), 1)
            v.tensor_copy(s1rows[:, :, :], ps[1][0:NB, 0:3 * 64].bitcast(BF16).rearrange("a (k p) -> a k p", k=3)
                          ).then_inc(s("s1_rows"), 1)
            dve.wait_ge(s("windows"), G // 2)
            link(v.tensor_copy(s1f[:, :], ps[7][:, 0:G]))
            split3(s1w, s1f[:, :], selC[:, 0:G])

            lookups(1, selC)
            dve.wait_ge(s("selected"), 2 * G + 1)
            v.memset(eC[:, T:TP], 0.0)
            link(v.tensor_tensor(eC[:, 0:T], eC[:, 0:T], selC[:, 0:T], ALU.add))
            v.scalar_tensor_tensor(eC[:, 0:T], eC[:, 0:T], SLOPE, eC[:, 0:T], ALU.mult, ALU.max).then_inc(s("e_cols"), 1)
            for h in range(2):
                n = min(4, EB - 4 * h)
                dve.wait_ge(s("e_turned"), h + 1)
                v.tensor_copy(rowF[:, 0, 4 * h:4 * h + n, :], ps[h][:, 0:n * P].rearrange("p (b t) -> p b t", t=P)).then_inc(s("e_rows"), 1)

            nscan = [0]

            def run_scan(out_, data, pen, op0, op1, neutral, reverse):
                n = nscan[0]
                nscan[0] += 1
                d, p_, o = (a[:, ::-1] if reverse else a for a in (data, pen, out_))
                v.tensor_tensor_scan(o, p_, d, neutral, op0, op1).then_inc(s("dve_step"), 1)
                steps[0] += 1
                link(v.tensor_reduce(lend[0:LP, 1:2], pen, AX.X, ALU.min))
                end = 0 if reverse else LW - 1
                v.tensor_copy(lend[0:LP, 0:1], out_[:, end:end + 1]).then_inc(s("ends_made"), 1)
                dve.wait_ge(s("ends_turned"), n + 1)
                link(v.tensor_copy(lrow[:, :, 0:LP], ps[6][0:1, 0:2 * P].rearrange("a (k p) -> a k p", k=2)[:, :, 0:LP]))
                link(v.memset(lcar[:, :], neutral))
                r0, r1, rc = lrow[0:1, 0, 0:LP], lrow[0:1, 1, 0:LP], lcar[0:1, 1:LP + 1]
                if reverse:
                    r0, r1, rc = r0[:, ::-1], r1[:, ::-1], rc[:, ::-1]
                v.tensor_tensor_scan(rc, r1, r0, neutral, op0, op1).then_inc(s("carry_made"), 1)
                dve.wait_ge(s("carry_turned"), n + 1)
                link(v.tensor_copy(lini[0:LP, :], ps[7][0:LP, 0:1]))
                link(v.tensor_tensor_scan(o, p_, d, lini[0:LP, 0:1], op0, op1))

            dve.wait_ge(s("e_loaded"), 16)
            run_scan(mL, eL, penL[:, :], ALU.add, ALU.max, -BIG, False)
            run_scan(tL, mL, penN[:, :], ALU.add, ALU.max, -BIG, True)
            v.tensor_tensor(eL, eL, tL, ALU.subtract).then_inc(s("e_shifted"), 1)
            dve.wait_ge(s("e_exp"), 1)
            run_scan(mL, eL, sameL[:, :], ALU.mult, ALU.add, 0.0, False)
            run_scan(tL, mL, penN[:, :], ALU.add, ALU.max, -BIG, True)
            link(v.reciprocal(tL, tL))
            link(v.memset(rowF[:, 0, EB - 1, :], 0.0))
            v.tensor_tensor(mL, eL, tL, ALU.mult).then_inc(s("alpha_made"), 1)
            for h in range(2):
                n = min(4, EB - 4 * h) * P
                dve.wait_ge(s("alpha_turned"), h + 1)
                link(v.tensor_copy(eC[:, 4 * P * h:4 * P * h + n], ps[h][:, 0:n]))
            v.memset(acc[:, :, :], 0.0).then_inc(s("acc_added"), 1)
            edge_pass(2, eC)

            dve.wait_ge(s("acc_added"), 3 * G + 3)
            dve.sem_inc(s("fin_free"), 3)
            dve.sem_inc(s("out_made"), 1)
            with dve.Fori(0, NCH) as c:
                dve.wait_ge(s("out_made"), c + 1)
                for b in range(NC):
                    dve.wait_ge(s("fin_prod"), c * NC + (b + 1))
                    v.scalar_tensor_tensor(u[:, b, :], ps[4 + b % 4][:, 0:D], 0.0, xsb[:, c * NC + b, :], ALU.max, ALU.add
                                           ).then_inc(s("fin_free"), 1)
                for b in range(NC):
                    dve.wait_ge(s("fin_free"), c * NC + (b + 4))
                    v.bn_stats(bst[:, b, :], u[:, b, :]).then_inc(s("fin_bn"), 1)
                dve.wait_ge(s("fin_bn"), c * NC + NC)
                dve.sem_inc(s("dve_passed"))
                for b in range(NC):
                    last = v.bn_aggr(mv[:, b, :], bst[:, b, :])
                last.then_inc(s("fin_stats"), 1)
                dve.wait_ge(s("fin_root"), c + 1)
                v.reciprocal(rs[:, :], sd[:, :]).then_inc(s("fin_rs"), 1)
                dve.wait_ge(s("fin_rs"), c + 1)
                for b in range(NC):
                    last = v.tensor_scalar(xsb[:, c * NC + b, :], u[:, b, :], mv[:, b, 0:1], rs[:, b:b + 1], ALU.subtract, ALU.mult)
                last.then_inc(s("out_made"), 1)


_INS = ['x', 'src', 'dst', 'edge_attr_128', 'edge_weight', 'L0_gnn_W1', 'L0_gnn_b1', 'L0_gnn_W2', 'L0_gnn_b2', 'L1_gnn_fc_w', 'L1_gnn_fc_r_w', 'L1_gnn_attn_w', 'L1_gnn_loop_w']
_OUTS = [((6250, 128), 'float32')]


def kernel(**inputs):
    import numpy as _np
    import concourse.bacc as _bacc
    from concourse import mybir as _mybir
    from concourse.bass_utils import run_bass_kernel_spmd as _run

    nc = _bacc.Bacc("TRN2", target_bir_lowering=False, num_devices=1)
    arrays, args = {}, []
    for name in _INS:
        a = _np.ascontiguousarray(inputs[name])
        arrays[f"in_{name}_dram"] = a
        args.append(nc.dram_tensor(f"in_{name}_dram", a.shape, _mybir.dt.from_np(a.dtype), kind="ExternalInput").ap())
    for i, (shape, dtype) in enumerate(_OUTS):
        dt = _mybir.dt.from_np(_np.dtype(dtype))
        args.append(nc.dram_tensor(f"out_{i}_dram", shape, dt, kind="ExternalOutput").ap())
    build(nc, *args)
    r = _run(nc, [arrays], core_ids=[0])
    got = tuple(r.results[0][f"out_{i}_dram"] for i in range(len(_OUTS)))
    return got[0]
```

```python
import concourse.bass as bass
from concourse import mybir
from contextlib import ExitStack

FP32 = mybir.dt.float32
BF16 = mybir.dt.bfloat16
I32 = mybir.dt.int32
ALU = mybir.AluOpType
ACT = mybir.ActivationFunctionType
AX = mybir.AxisListType
DVE, PE = mybir.EngineType.DVE, mybir.EngineType.PE

N, E, D = 6250, 100000, 128
P = 128
W = 128
GT = 8
GE = GT * P
G = -(-E // GE)
T = G * GT
EB = -(-T // P)
TP = EB * P
HG = G // 2
UG = 14
IT = G // UG
RG = 7
RTN = G // RG
RT = RG * GT
BACK = (0, 1, 2, 0, 1, 2, 3)
NBACK = max(BACK) + 1
RHS = (0, 1, 2, 3, 4) * 2 + (0, 1, 2, 3)
NRH = max(RHS) + 1
RS = RG + NBACK + NRH - 2
CREDIT = 16
NB = -(-N // P)
NC = 7
NCH = NB // NC
ACT_OH = 2
NV = 4
FB = 3 * NC
OUTB = (0, 1, 4, 5, 6, 7)
IDS = (0, 1, 0, 1, 0, 1, 0)
CB = 7
NP = NB // CB
DP = 5
AP = NP - DP
NLAST = N - (NB - 1) * P
NA = NB * P + W
FT = E // P
REST = FT - (EB - 1) * P
FR = E - FT * P
LP, LW = 125, 800
FAR = float(1 << 20)
BIG = 1.0e30
EPS = 1.0e-5
SLOPE = 0.01
assert G * GE == T * P and IT * UG == G and 2 * RG == UG and HG == RG * IT and TP - T >= RT and NCH * NC == NB and LP * LW == E


def build(nc, x, src, dst, edge_attr, edge_weight, W1, b1, W2, b2, fc_w, fc_r_w, attn_w, loop_w, out):
    ctx = ExitStack()
    with ctx:
        def sb(name, shape, dt=FP32):
            return ctx.enter_context(nc.sbuf_tensor(name, shape, dt))

        def sem(name):
            return ctx.enter_context(nc.semaphore(name))

        def scratch(name, shape, dt=FP32):
            return nc.dram_tensor(name, shape, dt).ap()

        parked_d = scratch("parked_d", (HG, P, GT * D))
        h1_d = scratch("h1_d", (NB * P, D))
        x2_d = scratch("x2_d", (NB * P, D))
        lo_d = scratch("lo_d", (TP * P,), BF16)
        rank_d = scratch("rank_d", (TP * P,), BF16)
        basef_d = scratch("basef_d", (EB * 16,))
        basei_d = scratch("basei_d", (EB * 16,), I32)
        s1_d = scratch("s1_d", (3, NB * P), BF16)
        deg_d = scratch("deg_d", (3, NB * P))
        e_d = scratch("e_d", (TP * P,))
        al_d = scratch("al_d", (E,))

        iota_i = sb("iota_i", [P, P], I32)
        pidx_i = sb("pidx_i", [P, 1], I32)
        iota = sb("iota", [P, P])
        iota_h = sb("iota_h", [P, P], BF16)
        pidx = sb("pidx", [P, 1])
        ident = sb("ident", [P, P])
        ident_h = sb("ident_h", [P, P], BF16)
        ones_h = sb("ones_h", [P, 1], BF16)
        ones = sb("ones", [P, 1])
        flag = sb("flag", [1, 1], I32)
        wide_e = sb("wide_e", [P, 3, GT])
        lrow0 = wide_e[0:1, 0, 0:1]
        iow = sb("iow", [P, 1])
        stageW = sb("stageW", [P, GT], I32)
        acc = sb("acc", [P, 2, NA])
        rows = acc[:, 1, 0:NB * D].rearrange("p (b d) -> p b d", d=D)
        erow = acc[:, 1, 0:7 * TP].rearrange("p (a b t) -> p a b t", a=7, t=P)
        srcR, dstR, loI = (erow[:, k].bitcast(I32) for k in range(3))
        ewR, rowF = erow[:, 3], erow[:, 4:7]
        s1P = acc[:, 1, 0:NA // 2].bitcast(BF16)
        loH = sb("loH", [P, EB, P], BF16)
        lin = acc[0:LP, 0, 0:6 * LW].rearrange("p (k j) -> p k j", k=6)
        dL, dprevL, dnextL = (lin[:, k].bitcast(I32) for k in range(3))
        eL, mL, tL = (lin[:, k] for k in range(3))
        tabf, s1f = acc[:, 0, 0:NB], acc[:, 0, 64:64 + G]
        s1p = acc[:, 0, 256:256 + 3 * 32].bitcast(BF16).rearrange("p (k b) -> p k b", k=3)[:, :, 0:NB]
        s1w = acc[:, 0, 512:512 + 3 * 64].bitcast(BF16).rearrange("p (k b) -> p k b", k=3)[:, :, 0:G]
        s1rows = acc[0:NB, 0, 1024:1024 + 3 * P // 2].bitcast(BF16).rearrange("a (k p) -> a k p", k=3)
        tab = acc[:, 1, 5400:5400 + 3 * 32].bitcast(BF16).rearrange("p (k b) -> p k b", k=3)[:, :, 0:NB]
        prod = acc[:, 1, 5500:5500 + GT * NB].rearrange("p (t a) -> p t a", a=NB)
        sameL = sb("sameL", [LP, LW], BF16)
        penL = sb("penL", [LP, LW], BF16)
        penN = sb("penN", [LP, LW], BF16)
        srcC = sb("srcC", [P, TP], I32)
        hiC = sb("hiC", [P, TP])
        rankC = sb("rankC", [P, TP])
        ewC = sb("ewC", [P, TP])
        t2C = sb("t2C", [P, TP])
        eC = t2C
        dmin = sb("dmin", [P, EB])
        base7 = sb("base7", [EB, 16])
        base7i = sb("base7i", [EB, 16], I32)
        baseB = sb("baseB", [P, EB * 16])
        base_row = sb("base_row", [1, EB * 16], I32)
        stage = sb("stage", [P, 2, RT], I32)
        ring = sb("ring", [P, RS, GT, D])
        S = sb("S", [P, 2, GT, W])
        SH = S[:, :, :, :].bitcast(BF16)
        far = t2C[:, 0:2 * ACT_OH * W // 2].bitcast(BF16).rearrange("p (a k w) -> p a k w", a=2, w=W)
        ewS = sb("ewS", [P, 2, GT, 3], BF16)
        xsb = sb("xsb", [P, NB, D])
        x2T = sb("x2T", [P, NA])
        deg3 = x2T[0:3, :]
        dinv = sb("dinv", [P, NB])
        dtmp = sb("dtmp", [P, 2, NB])
        rh = sb("rh", [P, 2, GT, D])
        rhH = rh[:, :, :, :].rearrange("p a t d -> p (a t d)").bitcast(BF16)
        ewP = rhH[:, 0:TP * 3].rearrange("p (t k) -> p t k", k=3)
        fcw, fcrw, lw, a2B = (rh[:, 1, 4 + k, :] for k in range(4))
        loB, rankB = (rhH[:, k * 2 * GE:(k + 1) * 2 * GE].rearrange("p (a n) -> p a n", a=2) for k in range(2))
        S1 = S[:, :, :, :].rearrange("p a t w -> p (a t w)")
        ohL, ohR = (S1.bitcast(BF16)[:, k * 2 * GE:(k + 1) * 2 * GE].rearrange("p (a n) -> p a n", a=2) for k in range(2))
        degR = S1[0:NB, 0:3 * P].rearrange("b (k p) -> b k p", p=P)
        u = S1[:, 0:NC * D].rearrange("p (b d) -> p b d", d=D)
        w1 = sb("w1", [P, D])
        w2 = sb("w2", [P, D])
        aw3 = sb("aw3", [3, D])
        awT = sb("awT", [P, 3])
        fcwT = sb("fcwT", [P, D])
        fcrwT = sb("fcrwT", [P, D])
        wz = sb("wz", [P, D])
        v01 = sb("v01", [P, 2])
        v2B = sb("v2B", [P, D])
        b1B = sb("b1B", [P, D])
        b2B = sb("b2B", [P, D])
        bst = sb("bst", [P, NB, 6])
        mv = sb("mv", [P, NB, 2])
        sd = sb("sd", [P, NB])
        rs = sb("rs", [P, NB])
        nmr = sb("nmr", [P, NB])
        pre1 = rows
        pre2 = ring[:, :, :, :].rearrange("p s t d -> p (s t) d")[:, 0:NB, :]
        epsc = sb("epsc", [P, 1])
        selC = ewC
        ends = 6 * LW
        lend, lini = acc[:, 0, ends:ends + 2], acc[:, 0, ends + 2:ends + 3]
        lrow = acc[0:1, 0, ends + 4:ends + 4 + 2 * P].rearrange("a (k p) -> a k p", k=2)
        lcar = acc[0:1, 0, ends + 4 + 2 * P:ends + 6 + 3 * P]

        ps = [ctx.enter_context(nc.psum_tensor(f"ps{k}", [P, 512], FP32)) for k in range(8)]

        sems = {}

        def s(name):
            if name not in sems:
                sems[name] = sem(name)
            return sems[name]

        ids = x2T[:, 0:2 * P].bitcast(I32).rearrange("p (a e) -> p a e", a=2)
        away = x2T[:, 2 * P:3 * P]
        blk0 = x2T[:, 3 * P:3 * P + NB]
        nblk0 = x2T[:, 3 * P + 64:3 * P + 64 + NB]
        ohV, ohA = (x2T[:, (4 + 2 * k * CB) * P:(4 + 2 * (k + 1) * CB) * P].rearrange("p (a b e) -> p a b e", a=2, e=P) for k in range(2))
        farA = x2T[:, (4 + 4 * CB) * P:(4 + 4 * CB) * P + CB * P // 2].bitcast(BF16).rearrange("p (b e) -> p b e", e=P)
        rhv = [rh[:, 0], rh[:, 1]] + [ring[:, RG + NBACK + k] for k in range(NRH - 2)]
        gathered = [sem(f"gathered{j}") for j in range(RG)]
        parked = [sem(f"parked{j}") for j in range(RG)]
        reloaded = [sem(f"reloaded{j}") for j in range(NBACK)]
        X2_MADE = (s("x2_made"), 1), (s("x2_made_act"), 1)
        rh_loaded = [sem(f"rh_loaded{j}") for j in range(2)]
        rh2_loaded = [sem(f"rh2_loaded{j}") for j in range(NRH)]
        ids_loaded = [sem(f"ids_loaded{j}") for j in range(2)]
        lo_loaded = [sem(f"lo_loaded{j}") for j in range(2)]
        rank_loaded = [sem(f"rank_loaded{j}") for j in range(2)]
        block = ctx.enter_context(nc.Block())

        def summed_by(p, n):
            return CREDIT + p * G + n

        def group(p, it, j):
            if p == 1:
                return it * UG + j, j % RG
            pair, fresh = divmod(j, 2)
            return it * RG + (pair + HG * fresh), pair if fresh else RG + BACK[pair % RG]

        def from_pool(p, q, k):
            return not (p == 1 and k == 0 and q % 2)

        def landed(p, slot, turns):
            return sum(16 for pp in range(p + 1) for t in range(turns if pp == p else RTN) for k in range(GT)
                       if from_pool(pp, t * RG + slot, k))

        def last_like(a, n):
            return n - 1 - (n - 1 - a) % 2

        def last_use(seq, j):
            return next(d for d in range(1, len(seq) + 1) if seq[(j - d) % len(seq)] == seq[j])

        def out_bank(r):
            return ps[OUTB[r % len(OUTB)]][:, r // len(OUTB) * P:(r // len(OUTB) + 1) * P]

        def bases(eng, q, n):
            _, regs = nc.values_load_multi_w_load_instructions(base_row[0:1, bass.ds(q, n)], engines=(eng,),
                                                               min_val=0, max_val=N - 1)
            return regs

        def any_wide(eng):
            eng.wait_ge(s("flag_made"), 1)
            return eng.If(eng.value_load(flag[0:1, 0:1], min_val=0, max_val=1) != 0)

        def ecols(q, n=GT):
            return bass.ds(q * GT, n)

        def erows(ap, first, n):
            return ap[first * P:(first + n) * P].rearrange("(t p) -> t p", p=P)

        @block.sync
        def _(sp):
            sp.wait_ge(s("pads_set"), 6)
            for dram, tile, loaded in ((src, srcR, s("src_loaded")), (dst, dstR, s("dst_loaded")), (edge_weight, ewR, s("ew_loaded"))):
                for b in range(EB - 1):
                    sp.dma_start(tile[:, b, :], erows(dram, b * P, P)).then_inc(loaded, 16)
                sp.dma_start(tile[0:REST, EB - 1, :], erows(dram, (EB - 1) * P, REST)).then_inc(loaded, 16)
                sp.dma_start(tile[REST:REST + 1, EB - 1, 0:FR],
                             dram[FT * P:E].rearrange("(a n) -> a n", a=1)).then_inc(loaded, 16)
            for tile, p0, p1, j0, j1, e0 in ((dL, 0, LP, 0, LW, 0), (dprevL, 0, 1, 1, LW, 0), (dprevL, 1, LP, 0, LW, LW - 1),
                                             (dnextL, 0, LP - 1, 0, LW, 1), (dnextL, LP - 1, LP, 0, LW - 1, E - LW + 1)):
                n = (p1 - p0) * (j1 - j0)
                sp.dma_start(tile[p0:p1, j0:j1], dst[e0:e0 + n].rearrange("(p j) -> p j", p=p1 - p0)
                             ).then_inc(s("lin_loaded"), 16)
            for b in range(0, NB - 1, 8):
                sp.dma_start(xsb[:, b:b + 8, :], x[b * P:(b + 8) * P, :].rearrange("(b p) d -> p b d", p=P)
                             ).then_inc(s("x_loaded"), 16)
            sp.dma_start(xsb[0:NLAST, NB - 1, :], x[(NB - 1) * P:N, :]).then_inc(s("x_loaded"), 16)
            for dram, tile in ((W1, w1), (W2, w2), (fc_w, fcw), (fc_r_w, fcrw), (loop_w, lw)):
                sp.dma_start(tile[:, :], dram[:, :]).then_inc(s("weights_loaded"), 16)
            sp.dma_start(aw3[:, :], attn_w.rearrange("a (k d) -> (a k) d", k=3)).then_inc(s("weights_loaded"), 16)
            for dram, tile in ((b1, b1B), (b2, b2B)):
                sp.dma_start(tile[:, :], dram.rearrange("(a d) -> a d", a=1).broadcast_to([P, D])
                             ).then_inc(s("weights_loaded"), 16)
            sp.wait_ge(s("base_made"), 2)
            sp.dma_start(basef_d.rearrange("(a g) -> a g", g=16), base7[:, :]).then_inc(s("base_stored"), 16)
            sp.dma_start(basei_d.rearrange("(a g) -> a g", g=16), base7i[:, :]).then_inc(s("base_stored"), 16)
            sp.wait_ge(s("base_stored"), 32)
            sp.dma_start(baseB[:, :], basef_d.rearrange("(a g) -> a g", a=1).broadcast_to([P, EB * 16])
                         ).then_inc(s("base_loaded"), 16)
            sp.dma_start(base_row[:, :], basei_d.rearrange("(a g) -> a g", a=1)).then_inc(s("base_loaded"), 16)
            sp.wait_ge(s("lo_made"), 1)
            sp.dma_start(lo_d.rearrange("(b t p) -> t b p", t=P, p=P), loH[:, :, :]).then_inc(s("lo_stored"), 16)
            sp.wait_ge(s("rank_rows"), 2)
            sp.dma_start(rank_d.rearrange("(b t p) -> t b p", t=P, p=P), loH[:, :, :]).then_inc(s("lo_stored"), 16)

            def store_chunks(table, made, stored, rows=rows):
                with sp.Fori(0, NCH) as c:
                    for m, n in made:
                        sp.wait_ge(m, c * n + n)
                    sp.dma_start(table[bass.ds(c * NC * P, NC * P), :].rearrange("(b p) d -> p b d", p=P),
                                 rows[:, bass.ds(c * NC, NC), :]).then_inc(stored, 16)

            def park(r):
                with sp.Fori(0, RG) as t:
                    for j in range(RG):
                        sp.wait_ge(gathered[j], t * (16 * GT) + landed(2 * r, j, 1))
                        sp.dma_start(parked_d[bass.ds(t * RG + j, 1), :, :].rearrange("a p n -> (a p) n"),
                                     ring[:, j, :, :]).then_inc(parked[j], 16)
                for j in range(RG):
                    sp.wait_ge(parked[j], 16 * RG * (r + 1))

            def reload(p, t, j):
                sp.wait_ge(s("summed"), t * UG + (summed_by(p, 1) + 2 * (j - last_use(BACK, j))))
                sp.dma_start(ring[:, RG + BACK[j], :, :], parked_d[bass.ds(t * RG + j, 1), :, :].rearrange("a p n -> (a p) n")
                             ).then_inc(reloaded[BACK[j]], 16)

            park(0)
            with sp.Fori(0, IT) as t:
                for j in range(RG):
                    reload(0, t, j)

            def rh_rows(q, n=GT):
                return edge_attr[bass.ds(q * GE, n * P), :].rearrange("(t p) d -> p t d", p=P)

            def load_last_rh(tile, loaded, tails):
                sp.dma_start(tile[0:FR, FT - (G - 1) * GT, :], edge_attr[FT * P:E, :]).then_inc(s("tail_loaded"), 16)
                sp.wait_ge(s("tail_loaded"), 16 * tails)
                sp.dma_start(tile[:, 0:FT - (G - 1) * GT, :], rh_rows(G - 1, FT - (G - 1) * GT)).then_inc(loaded, 16)

            store_chunks(h1_d, [(s("h1_made"), NC)], s("h1_stored"))
            for j in range(2):
                sp.wait_ge(lo_loaded[j], 16 * (G // 2 + 1))
            def load_ids(t, j, q):
                sp.wait_ge(s("ids_used"), t * RG + (j + 4 - last_use(IDS, j)))
                sp.dma_start(ids[:, IDS[j], :], src[bass.ds(q * GE, P)].rearrange("(a e) -> a e", a=1).broadcast_to([P, P])
                             ).then_inc(ids_loaded[IDS[j]], 16)

            def load_pair1(t, j, last=False):
                load_ids(t, j, 1 if last else t * UG + (2 * j + 3))
                for h in range(2):
                    n = 2 * j + h
                    sp.wait_ge(s("rh_dotted"), t * UG + (n + 1))
                    if last and h:
                        load_last_rh(rh[:, 1], rh_loaded[1], 1)
                    else:
                        sp.dma_start(rh[:, h], rh_rows(t * UG + n)).then_inc(rh_loaded[h], 16)

            load_ids(0, -1, 1)
            with sp.Fori(0, IT - 1) as t:
                for j in range(RG):
                    load_pair1(t, j)
            for j in range(RG):
                load_pair1(IT - 1, j, j == RG - 1)
            store_chunks(x2_d, X2_MADE, s("x2_stored"), xsb)
            park(1)
            sp.wait_ge(s("selected"), 2 * G + 1)
            for j in range(2):
                sp.wait_ge(lo_loaded[j], 16 * (G + 2))
                sp.wait_ge(rank_loaded[j], 16 * (G // 2 + 1))

            def load_pair(t, j, last=False):
                reload(2, t, j)
                for h in range(2):
                    n = 2 * j + h
                    q, _ = group(2, t, n)
                    sp.wait_ge(s("summed"), t * UG + (summed_by(2, 1) + n - last_use(RHS, n)))
                    if last and h:
                        load_last_rh(rhv[RHS[n]], rh2_loaded[RHS[n]], 2)
                    else:
                        sp.dma_start(rhv[RHS[n]], rh_rows(q)).then_inc(rh2_loaded[RHS[n]], 16)

            with sp.Fori(0, IT - 1) as t:
                for j in range(RG):
                    load_pair(t, j)
            for j in range(RG):
                load_pair(IT - 1, j, j == RG - 1)
            with any_wide(sp):
                sp.wait_ge(s("summed"), summed_by(2, G))
                with sp.Fori(0, G - 1) as g:
                    sp.wait_ge(s("wide_group"), g + (3 * G + 1))
                    sp.dma_start(rh[:, 0], rh_rows(g)).then_inc(s("wide_rh"), 16)
                sp.wait_ge(s("wide_group"), 4 * G)
                load_last_rh(rh[:, 0], s("wide_rh"), 3)
            with sp.Fori(0, NCH - 1) as c:
                sp.wait_ge(s("out_made"), c + 2)
                sp.dma_start(out[bass.ds(c * NC * P, NC * P), :].rearrange("(b p) d -> p b d", p=P),
                             xsb[:, bass.ds(c * NC, NC), :]).then_inc(s("out_stored"), 16)
            sp.wait_ge(s("out_made"), NCH + 1)
            sp.dma_start(out[(NCH - 1) * NC * P:(NB - 1) * P, :].rearrange("(b p) d -> p b d", p=P),
                         xsb[:, (NCH - 1) * NC:NB - 1, :]).then_inc(s("out_stored"), 16)
            sp.dma_start(out[(NB - 1) * P:N, :], xsb[0:NLAST, NB - 1, :]).then_inc(s("out_stored"), 16)
            sp.wait_ge(s("out_stored"), 16 * (NCH + 1))

        @block.gpsimd
        def _(pool):
            nc.gpsimd.memset(srcR[:, EB - 1, :], 0).then_inc(s("pads_set"), 1)
            nc.gpsimd.memset(dstR[:, EB - 1, :], int(FAR)).then_inc(s("pads_set"), 1)
            nc.gpsimd.memset(ewR[:, EB - 1, :], 0.0).then_inc(s("pads_set"), 1)
            nc.gpsimd.memset(xsb[:, NB - 1, :], 0.0).then_inc(s("pads_set"), 1)
            nc.gpsimd.memset(dprevL[:, 0:LW], -1).then_inc(s("pads_set"), 1)
            nc.gpsimd.memset(dnextL[:, 0:LW], -1).then_inc(s("pads_set"), 1)
            nc.gpsimd.iota(iota_i[:, :], [[1, P]], base=0, channel_multiplier=0).then_inc(s("iota_made"), 1)
            nc.gpsimd.iota(pidx_i[:, :], [[1, 1]], base=0, channel_multiplier=1).then_inc(s("iota_made"), 1)
            nc.gpsimd.memset(acc[:, 0, NB * P:NA], 0.0).then_inc(s("tails_set"), 1)
            nc.gpsimd.memset(x2T[:, :], 0.0).then_inc(s("tails_set"), 1)
            nc.gpsimd.memset(ones_h[:, :], 1.0).then_inc(s("tails_set"), 1)
            nc.gpsimd.memset(ones[:, :], 1.0).then_inc(s("tails_set"), 1)
            nc.gpsimd.memset(epsc[:, :], EPS).then_inc(s("tails_set"), 1)

            def turn(p, table, t, half, free, before):
                pool.wait_ge(s("staged"), t + (p * RTN + 1))
                for j in range(RG):
                    if free:
                        pool.wait_ge(*free(j))
                    pool.sem_inc(s("pool_passed"))
                    for k in range(GT):
                        if not from_pool(p, half * RG + j, k):
                            continue
                        c = j * GT + k
                        pool.indirect_dma_start(
                            ring[:, j, k, :], None, table[:, :],
                            bass.IndirectOffsetOnAxis(ap=stage[:, half, c:c + 1], axis=0)).then_inc(gathered[j], 16)
                    if j == RG // 2:
                        for m in range(RG):
                            if before:
                                pool.wait_ge(gathered[m], before(m))
                        pool.sem_inc(s("pool_passed"))
                        nc.gpsimd.tensor_copy(stage[:, 1 - half, :], srcC[:, bass.ds(t * RT + RT, RT)]).then_inc(s("staged"), 1)

            def parked_pass(p, table):
                r = p // 2
                turn(p, table, 0, 0, None, p and (lambda m: landed(p, m, 0)))
                with pool.Fori(0, RG // 2) as i:
                    for h in range(2):
                        turn(p, table, i * 2 + (1 + h), 1 - h, lambda j: (parked[j], i * 32 + 16 * (r * RG + 1 + h)),
                             lambda m: i * (2 * 16 * GT) + landed(p, m, 1 + h))
                turn(p, table, RG, 1, lambda j: (parked[j], 16 * RG * (r + 1)), lambda m: landed(p, m, RG))
                with pool.Fori(0, RG // 2) as i:
                    for h in range(2):
                        turn(p, table, i * 2 + (RG + 1 + h), h,
                             lambda j: (s("summed"), i * (2 * UG) + (summed_by(p, 2 * j + 2) + h * UG)),
                             lambda m: i * (2 * 16 * GT) + landed(p, m, RG + 1 + h))

            def wide_gathers(p, table):
                pool.wait_ge(s("summed"), summed_by(p, G))
                with any_wide(pool):
                    with pool.Fori(0, G) as g:
                        pool.wait_ge(s("wide_group"), g + ((p + 1) * G + 1))
                        pool.sem_inc(s("pool_passed"))
                        nc.gpsimd.tensor_copy(stageW[:, :], srcC[:, ecols(g)]).then_inc(s("wide_staged"), 1)
                        pool.wait_ge(s("wide_staged"), g + (p * G + 1))
                        pool.sem_inc(s("pool_passed"))
                        for k in range(GT):
                            pool.indirect_dma_start(
                                ring[:, 0, k, :], None, table[:, :],
                                bass.IndirectOffsetOnAxis(ap=stageW[:, k:k + 1], axis=0)).then_inc(s("wide_gathered"), 16)

            pool.wait_ge(s("src_cols"), 1)
            nc.gpsimd.tensor_copy(stage[:, 0, :], srcC[:, 0:RT]).then_inc(s("staged"), 1)
            parked_pass(0, x)
            wide_gathers(0, x)
            pool.wait_ge(s("h1_stored"), 16 * NCH)
            with pool.Fori(0, RTN // 2) as i:
                for h in range(2):
                    turn(1, h1_d, i * 2 + h, h, lambda j: (s("summed"), i * UG + (summed_by(1, j + 1) + (h - 1) * RG)),
                         lambda m: i * (landed(1, m, 2) - landed(1, m, 0)) + landed(1, m, h))
            wide_gathers(1, h1_d)
            for b in range(NB):
                pool.wait_ge(s("l2_sigm"), b + 1)
                nc.gpsimd.tensor_tensor(pre1[:, b, :], pre1[:, b, :], xsb[:, b, :], ALU.add).then_inc(s("l2_res"), 1)
            pool.wait_ge(s("x2_stored"), 16 * NCH)
            parked_pass(2, x2_d)
            wide_gathers(2, x2_d)

        @block.tensor
        def _(pe):
            nbatch = 0
            pe.wait_ge(s("ident_made"), 1)

            def rows_to_cols(tile, ready, count):
                nonlocal nbatch
                pe.wait_ge(ready, count)
                for h in range(2):
                    if nbatch >= 2:
                        pe.wait_ge(s("cols_copied"), nbatch - 1)
                    n = min(4, EB - 4 * h)
                    for b in range(n):
                        last = nc.tensor.transpose(ps[nbatch % 2][:, b * P:(b + 1) * P], tile[:, 4 * h + b, :], ident[:, :])
                    last.then_inc(s("cols_ready"), 1)
                    nbatch += 1

            rows_to_cols(rowF[:, 1], s("rowF_made"), 1)
            rows_to_cols(rowF[:, 2], s("rowF_made"), 2)
            rows_to_cols(rowF[:, 0], s("rowF_made"), 3)
            pe.wait_ge(s("dmin_made"), 1)
            nc.tensor.transpose(ps[2][0:EB, 0:P], dmin[:, :], ident[:, :]).then_inc(s("dmin_turned"), 1)
            rows_to_cols(ewR, s("ew_loaded"), 16 * (EB + 1))
            pe.wait_ge(s("wide_found"), 1)
            nc.tensor.transpose(ps[2][0:1, 0:P], dmin[:, 0:1], ident[:, :]).then_inc(s("wide_turned"), 1)
            pe.wait_ge(s("weights_loaded"), 16 * 8)
            nc.tensor.transpose(ps[3][:, 0:P], fcw[:, :], ident[:, :])
            nc.tensor.transpose(ps[3][:, P:2 * P], fcrw[:, :], ident[:, :])
            nc.tensor.matmul(ps[3][:, 2 * P:3 * P], fcw[:, :], lw[:, :], start=True, stop=True)
            nc.tensor.transpose(ps[3][:, 3 * P:3 * P + 3], aw3[:, :], ident[0:3, 0:3]).then_inc(s("wprod"), 1)
            pe.wait_ge(s("awT_copied"), 2)
            nc.tensor.matmul(ps[4][:, 0:2], fcw[:, :], awT[:, 0:2], start=True, stop=True)
            nc.tensor.matmul(ps[4][:, P:2 * P], a2B[:, :], fcrw[:, :], start=True, stop=True).then_inc(s("wprod"), 1)
            pe.wait_ge(s("rank_made"), 1)
            for h in range(2):
                pe.wait_ge(s("cols_copied"), nbatch - 1)
                n = min(4, EB - 4 * h)
                for b in range(n):
                    last = nc.tensor.transpose(ps[nbatch % 2][:, b * P:(b + 1) * P],
                                               rankC[:, (4 * h + b) * P:(4 * h + b + 1) * P], ident[:, :])
                last.then_inc(s("cols_ready"), 1)
                nbatch += 1

            def wide_sums(ph, *rows_of):
                with pe.Fori(0, G) as g:
                    if ph:
                        pe.wait_ge(s("wide_gathered"), g * (16 * GT) + 16 * GT * ((ph - 1) * G + 1))
                    if ph == 3:
                        pe.wait_ge(s("wide_rh"), g * 16 + 16)
                    pe.sem_inc(s("pe_passed"))
                    with pe.Fori(0, NB) as r:
                        pe.wait_ge(s("wide_S"), g * NB + r + (ph * G * NB + 1))
                        for a, m, rows_k in rows_of:
                            for k in range(GT):
                                last = nc.tensor.matmul(ps[2][0:m, a * W:(a + 1) * W], rows_k(k), S[:, 0, k, :],
                                                        start=(k == 0), stop=(k == GT - 1))
                        last.then_inc(s("wide_summed"), 1)

            pe.sem_inc(s("deg_summed"), 2)
            with pe.Fori(0, G // 2) as i:
                for j in range(2):
                    pe.wait_ge(s("deg_onehot"), i * 2 + (j + 1))
                    pe.wait_ge(s("deg_onehot_act"), i * 2 + (j + 1))
                    for k in range(GT):
                        last = nc.tensor.matmul(ps[5 + j][0:3, 0:W], ewS[:, j, k, :], SH[:, j, k, 0:W],
                                                start=(k == 0), stop=(k == GT - 1))
                    last.then_inc(s("deg_summed"), 1)
            with any_wide(pe):
                wide_sums(0, (0, 1, lambda k: ones[:, 0:1]))
            pe.wait_ge(s("degR_loaded"), 16)
            for part in range(3):
                last = nc.tensor.matmul(ps[7][:, 0:NB], degR[:, part, :], ident[0:NB, 0:NB], start=(part == 0), stop=(part == 2))
            last.then_inc(s("deg_cols"), 1)
            for c in range(NCH):
                pe.wait_ge(s("x1_made"), c + 1)
                for b in range(NC):
                    if b % 4 == 0:
                        pe.wait_ge(s("x1_evac"), c * 2 + (b // 4 + 1))
                    last = nc.tensor.transpose(ps[b // 4][:, (b % 4) * P:(b % 4 + 1) * P],
                                               rows[:, c * NC + b, :], ident[:, :])
                    if b in (3, NC - 1):
                        last.then_inc(s("x1_turned"), 1)

            def lookups(r):
                with pe.Fori(0, G // 2) as i:
                    for j in range(2):
                        pe.wait_ge(s("onehot_built"), i * 2 + (j + 1 + r * (G + 1)))
                        for k in range(GT):
                            for part in range(3):
                                last = nc.tensor.matmul(ps[4 + j][:, 64 * k:64 * k + NB], ohL[:, j, k * P:(k + 1) * P], tab[:, part, :],
                                                        start=(part == 0), stop=(part == 2))
                        for k in range(GT if r else 0):
                            for part in range(3):
                                last = nc.tensor.matmul(ps[2 + j][:, k:k + 1], ohR[:, j, k * P:(k + 1) * P],
                                                        s1w[:, part, bass.ds(i * 2 + j, 1)], start=(part == 0), stop=(part == 2))
                        last.then_inc(s("looked_up"), 1)

            pe.sem_inc(s("summed"), CREDIT)
            pe.wait_ge(s("tables_split"), 1)
            lookups(0)

            def slot_loads(loaded, seq, it, j, before=0):
                uses = seq.count(seq[j])
                pe.wait_ge(loaded[seq[j]], it * (16 * uses) + 16 * (before * uses + seq[:j + 1].count(seq[j])))

            def sum_pass(p):
                with pe.Fori(0, IT) as it:
                    for j in range(UG):
                        _, slot = group(p, 0, j)
                        if p == 1:
                            pe.wait_ge(gathered[slot], it * (landed(1, slot, 2) - landed(1, slot, 0)) + landed(1, slot, j // RG + 1))
                        elif j % 2:
                            pe.wait_ge(gathered[slot], it * (16 * GT) + landed(p, slot, RG + 1))
                        else:
                            slot_loads(reloaded, BACK, it, j // 2, p // 2 * IT)
                        pe.wait_ge(s("S_built"), it * UG + (p * (G + 1) + j + 1))
                        if p == 1 and j % 2:
                            pe.wait_ge(s("assisted"), it * RG + (j // 2 + 2))
                        for k in range(GT):
                            last = nc.tensor.matmul(ps[2 + j % 2][:, 0:W], ring[:, slot, k, :], S[:, j % 2, k, :],
                                                    start=(k == 0), stop=(k == GT - 1))
                        if p == 2:
                            slot_loads(rh2_loaded, RHS, it, j)
                            for k in range(GT):
                                last = nc.tensor.matmul(ps[2 + j % 2][:, W:2 * W], rhv[RHS[j]][:, k, :], S[:, j % 2, k, :],
                                                        start=(k == 0), stop=(k == GT - 1))
                        last.then_inc(s("summed"), 1)
                        if p == 1:
                            pick_pieces(it, j // 2, range(DP, NP) if j % 2 else range(DP))

            def pick_pieces(it, m, pieces):
                if pieces[0] == 0:
                    pe.wait_ge(s("assisted"), it * RG + (m + 2))
                for c in pieces:
                    if c < DP:
                        pe.wait_ge(s("oh_built"), it * (RG * DP) + ((m + 1) * DP + c + 2))
                        piece = ohV[:, c % 2]
                    else:
                        pe.wait_ge(s("oh_built_act"), it * (RG * AP) + (AP + (m + 1) * AP + c - DP + 1))
                        piece = ohA[:, (c - DP) % 2]
                    for b in range(CB):
                        last = nc.tensor.matmul(ps[6][:, 0:D], piece[:, b, :], rows[:, c * CB + b, :],
                                                start=(c + b == 0), stop=(c == NP - 1 and b == CB - 1))
                    last.then_inc(s("oh_used"), 1)

            pe.sem_inc(s("oh_used"), NP)
            sum_pass(0)
            with any_wide(pe):
                wide_sums(1, (0, P, lambda k: ring[:, 0, k, :]))
            def layer(weight, ready, count, made, evac, turned, free, prod, rows=rows):
                pe.wait_ge(ready, count)
                for b in range(NB):
                    pe.wait_ge(free, b + 1)
                    nc.tensor.matmul(ps[4 + b % NC % 4][:, 0:D], acc[:, 0, b * P:(b + 1) * P], weight[:, :],
                                     start=True, stop=True).then_inc(prod, 1)
                for c in range(NCH):
                    for m, n in made:
                        pe.wait_ge(m, (c + 1) * n)
                    for b in range(NC):
                        if b % 4 == 0:
                            pe.wait_ge(evac, c * 2 + (b // 4 + 1))
                        last = nc.tensor.transpose(ps[b // 4][:, (b % 4) * P:(b % 4 + 1) * P],
                                                   rows[:, c * NC + b, :], ident[:, :])
                        if b in (3, NC - 1):
                            last.then_inc(turned, 1)

            layer(w1, s("sums_made"), 1, [(s("h1_made"), NC)], s("h1_evac"), s("h1_turned"), s("l1_free"), s("l1_prod"))
            pe.sem_inc(s("assisted"), 1)
            pick_pieces(0, -1, range(NP))
            sum_pass(1)
            with any_wide(pe):
                wide_sums(2, (0, P, lambda k: ring[:, 0, k, :]))
            pe.wait_ge(s("assisted"), HG + 2)
            layer(w2, s("sums_made"), 2, X2_MADE,
                  s("x2_evac"), s("x2_turned"), s("l2_free"), s("l2_prod"), xsb)
            pe.wait_ge(s("x2_evac"), 2 * NCH + 2)
            for b in range(NB):
                last = nc.tensor.matmul(ps[6][:, 2 * b:2 * b + 2], x2T[:, b * P:(b + 1) * P], v01[:, :], start=True, stop=True)
            last.then_inc(s("scores"), 1)
            pe.wait_ge(s("tables_split"), 2)
            for part in range(3):
                last = nc.tensor.transpose(ps[1][0:NB, part * 64:(part + 1) * 64].bitcast(BF16), s1p[:, part, :], ident_h[:, :])
            last.then_inc(s("s1_turned"), 1)
            pe.wait_ge(s("s1_loaded"), 16)
            with pe.Fori(0, IT) as it:
                first = bases(PE, it * UG, UG)
                for j in range(UG):
                    last = nc.tensor.matmul(ps[7][:, bass.ds(it * UG + j, 1)], s1P[:, bass.ds(first[j], W)], ones_h[:, :],
                                            start=True, stop=True)
                last.then_inc(s("windows"), 1)
            pe.wait_ge(s("tables_split"), 4)
            lookups(1)
            with any_wide(pe):
                with pe.Fori(0, NB) as r:
                    pe.wait_ge(s("wide_s1_used"), r + 1)
                    nc.tensor.matmul(ps[2][:, 0:P], S[:, 1, 0, :], x2T[:, bass.ds(r * P, P)], start=True, stop=True
                                     ).then_inc(s("wide_s1"), 1)
            pe.wait_ge(s("e_cols"), 1)
            for h in range(2):
                n = min(4, EB - 4 * h)
                for b in range(n):
                    last = nc.tensor.transpose(ps[h][:, b * P:(b + 1) * P], eC[:, (4 * h + b) * P:(4 * h + b + 1) * P], ident[:, :])
                last.then_inc(s("e_turned"), 1)
            for n in range(4):
                pe.wait_ge(s("ends_made"), n + 1)
                nc.tensor.transpose(ps[6][0:1, 0:LP], lend[0:LP, 0:1], ident[0:LP, 0:LP])
                nc.tensor.transpose(ps[6][0:1, P:P + LP], lend[0:LP, 1:2], ident[0:LP, 0:LP]).then_inc(s("ends_turned"), 1)
                pe.wait_ge(s("carry_made"), n + 1)
                off = 2 if n % 2 else 0
                nc.tensor.transpose(ps[7][0:LP, 0:1], lcar[0:1, off:off + LP], ident[0:1, 0:1]).then_inc(s("carry_turned"), 1)
            pe.wait_ge(s("alpha_loaded"), 16 * (EB + 1))
            for h in range(2):
                n = min(4, EB - 4 * h)
                for b in range(n):
                    last = nc.tensor.transpose(ps[h][:, b * P:(b + 1) * P], rowF[:, 0, 4 * h + b, :], ident[:, :])
                last.then_inc(s("alpha_turned"), 1)
            sum_pass(2)
            with any_wide(pe):
                wide_sums(3, (0, P, lambda k: ring[:, 0, k, :]), (1, P, lambda k: rh[:, 0, k, :]))
            pe.wait_ge(s("sums_made"), 3)
            for b in range(NB):
                bank, blk = out_bank(b % FB), slice(b * P, (b + 1) * P)
                before = [a for a in range(b) if a % FB % len(OUTB) == b % FB % len(OUTB)]
                if before:
                    pe.wait_ge(s("fin_free"), before[-1] + 1)
                nc.tensor.matmul(bank, x2T[:, blk], wz[:, :], start=True, stop=False)
                nc.tensor.matmul(bank, acc[:, 0, blk], fcwT[:, :], start=False, stop=False)
                nc.tensor.matmul(bank, acc[:, 1, blk], fcrwT[:, :], start=False, stop=True).then_inc(s("fin_prod"), 1)

        @block.scalar
        def _(act):
            act.wait_ge(s("flag_made"), 1)
            act.wait_ge(s("ew_split"), 1)
            with act.Fori(0, IT) as it:
                for j in range(UG):
                    q = it * UG + j
                    act.wait_ge(s("deg_summed"), it * UG + (j + 1))
                    act.sem_inc(s("act_passed"))
                    nc.scalar.copy(ewS[:, j % 2, :, :], ewP[:, ecols(q), :])
                    for k in range(GT - ACT_OH, GT):
                        last = nc.scalar.activation(far[:, j % 2, k - GT + ACT_OH, :], iota_h[:, :], ACT.Abs, scale=-1.0,
                                                    bias=rankC[:, bass.ds(q * GT + k, 1)])
                    last.then_inc(s("deg_far"), 1)
                    act.wait_ge(s("deg_far"), it * UG + (j + 1))
                    act.sem_inc(s("act_passed"))
                    nc.scalar.activation(SH[:, j % 2, GT - ACT_OH:GT, 0:W], far[:, j % 2, :, :], ACT.Relu, scale=-1.0, bias=1.0
                                         ).then_inc(s("deg_onehot_act"), 1)
            act.wait_ge(s("deg_made"), 1)
            act.dma_start(deg_d[:, :], deg3[:, 0:NB * P]).then_inc(s("deg_stored"), 16)
            act.wait_ge(s("deg_stored"), 16)
            act.dma_start(degR[:, :, :], deg_d[:, :].rearrange("k (b p) -> b k p", p=P)).then_inc(s("degR_loaded"), 16)
            act.wait_ge(s("deg_clamped"), 1)
            nc.scalar.activation(dtmp[:, 0, :], dtmp[:, 0, :], ACT.Sqrt).then_inc(s("deg_root"), 1)

            def evacuate(turned, evac, dest):
                with act.Fori(0, NCH) as c:
                    for h in range(2):
                        n = 4 if h == 0 else NC - 4
                        act.wait_ge(turned, c * 2 + (h + 1))
                        act.sem_inc(s("act_passed"))
                        nc.scalar.copy(dest[:, bass.ds(c * (NC * P) + h * 4 * P, n * P)], ps[h][:, 0:n * P]
                                       ).then_inc(evac, 1)

            evacuate(s("x1_turned"), s("x1_evac"), acc[:, 0, :])

            def load_lo(r):
                def one(q, j):
                    for dram, tile, loaded in ((lo_d, loB, lo_loaded[j]), (rank_d, rankB, rank_loaded[j]))[:1 + r]:
                        act.dma_start(tile[:, j, :], dram[bass.ds(q * GE, GE)].rearrange("(a n) -> a n", a=1)
                                      .broadcast_to([P, GE])).then_inc(loaded, 16)
                for j in range(2):
                    one(j, j)
                with act.Fori(1, G // 2 + 1) as i:
                    for j in range(2):
                        act.wait_ge(s("onehot_built"), i * 2 + (j - 1 + r * (G + 1)))
                        one(i * 2 + j, j)

            act.wait_ge(s("lo_stored"), 32)
            load_lo(0)
            for b in range(NB):
                act.wait_ge(s("l1_free"), b + 4)
                nc.scalar.activation(rows[:, b, :], u[:, b % NC, :], ACT.Relu, scale=dinv[:, b:b + 1]).then_inc(s("h1_made"), 1)
            evacuate(s("h1_turned"), s("h1_evac"), acc[:, 0, :])
            act.sem_inc(s("oh_built_act"), AP)
            act.wait_ge(s("blk0_made"), 1)

            def assist(it, m):
                n = m + 1
                act.wait_ge(s("ids_used"), it * RG + (n + 3))
                for a in range(AP):
                    c = DP + a
                    act.wait_ge(s("oh_used"), it * (RG * NP) + (NP + n * NP + (c - 1 if a > 1 else DP + last_like(a, AP) + 1 - NP)))
                    act.wait_ge(s("oh_built_act"), it * (RG * AP) + (AP + n * AP + a))
                    act.sem_inc(s("act_passed"))
                    for b in range(CB):
                        last = nc.scalar.activation(farA[:, b, :], away, ACT.Abs, bias=nblk0[:, c * CB + b:c * CB + b + 1])
                    last.then_inc(s("far_made"), 1)
                    act.wait_ge(s("far_made"), it * (RG * AP) + (n * AP + a + 1))
                    act.sem_inc(s("act_passed"))
                    nc.scalar.activation(ohA[:, a % 2, :, :], farA[:, :, :], ACT.Relu, scale=-1.0, bias=1.0
                                         ).then_inc(s("oh_built_act"), 1)
                _, slot = group(1, 0, 2 * n + 1)
                act.wait_ge(s("oh_used"), it * (RG * NP) + (n + 2) * NP)
                act.wait_ge(s("summed"), it * UG + (summed_by(1, 2 * n + 2) - RG))
                act.sem_inc(s("act_passed"))
                nc.scalar.copy(ring[:, slot, 0, :], ps[6][:, 0:D]).then_inc(s("assisted"), 1)

            assist(0, -1)
            with act.Fori(0, IT) as it:
                for m in range(RG):
                    assist(it, m)
            for b in range(NB):
                act.wait_ge(s("l2_free"), b + 4)
                nc.scalar.activation(pre1[:, b, :], pre1[:, b, :], ACT.Sigmoid).then_inc(s("l2_sigm"), 1)
            act.wait_ge(s("stats_made"), 1)
            nc.scalar.activation(sd[:, :], mv[:, :, 1], ACT.Sqrt, bias=epsc[:, 0:1]).then_inc(s("std_made"), 1)
            act.wait_ge(s("scale_made"), 1)
            for c in range(NCH):
                for b in range(c * NC + NV, (c + 1) * NC):
                    last = nc.scalar.activation(xsb[:, b, :], pre1[:, b, :], ACT.Identity, scale=rs[:, b:b + 1], bias=nmr[:, b:b + 1])
                last.then_inc(s("x2_made_act"), 1)
            evacuate(s("x2_turned"), s("x2_evac"), x2T[:, :])
            act.wait_ge(s("s1_rows"), 1)
            act.dma_start(s1_d[:, :].rearrange("k (a p) -> a k p", p=P), s1rows[:, :, :]).then_inc(s("s1_stored"), 16)
            act.wait_ge(s("s1_stored"), 16)
            act.wait_ge(s("s1_cleared"), 1)
            act.dma_start(s1P[0:3, 0:NB * P], s1_d[:, :]).then_inc(s("s1_loaded"), 16)
            load_lo(1)
            act.wait_ge(s("e_rows"), 2)
            act.dma_start(e_d.rearrange("(b t p) -> t b p", t=P, p=P), rowF[:, 0, :, :]).then_inc(s("e_stored"), 16)
            act.wait_ge(s("e_stored"), 16)
            act.dma_start(eL, e_d[0:E].rearrange("(p j) -> p j", p=LP)).then_inc(s("e_loaded"), 16)
            act.wait_ge(s("e_shifted"), 1)
            nc.scalar.activation(eL, eL, ACT.Exp).then_inc(s("e_exp"), 1)
            act.wait_ge(s("alpha_made"), 1)
            act.dma_start(al_d.rearrange("(p j) -> p j", p=LP), mL).then_inc(s("alpha_stored"), 16)
            act.wait_ge(s("alpha_stored"), 16)
            for b in range(EB - 1):
                act.dma_start(rowF[:, 0, b, :], erows(al_d, b * P, P)).then_inc(s("alpha_loaded"), 16)
            act.dma_start(rowF[0:REST, 0, EB - 1, :], erows(al_d, (EB - 1) * P, REST)).then_inc(s("alpha_loaded"), 16)
            act.dma_start(rowF[REST:REST + 1, 0, EB - 1, 0:FR], al_d[FT * P:E].rearrange("(a n) -> a n", a=1)
                         ).then_inc(s("alpha_loaded"), 16)
            for c in range(NCH):
                blks = slice(c * NC, (c + 1) * NC)
                act.wait_ge(s("stats_made"), c + 2)
                nc.scalar.activation(sd[:, blks], mv[:, blks, 1], ACT.Sqrt, bias=epsc[:, 0:1]).then_inc(s("std_made"), 1)
                act.wait_ge(s("scale_made"), c + 2)
                for b in range(c * NC, (c + 1) * NC):
                    last = nc.scalar.activation(xsb[:, b, :], pre2[:, b, :], ACT.Identity, scale=rs[:, b:b + 1], bias=nmr[:, b:b + 1])
                last.then_inc(s("out_made"), 1)

        @block.vector
        def _(dve):
            v = nc.vector
            steps = [0]

            def link(ins):
                steps[0] += 1
                ins.then_inc(s("dve_step"), 1)
                dve.wait_ge(s("dve_step"), steps[0])

            dve.wait_ge(s("iota_made"), 2)
            link(v.tensor_copy(pidx[:, :], pidx_i[:, :]))
            v.tensor_copy(iota_h[:, :], iota_i[:, :])
            link(v.tensor_copy(iota[:, :], iota_i[:, :]))
            v.tensor_scalar(ident_h[:, :], iota[:, :], pidx[:, 0:1], None, ALU.is_equal)
            v.tensor_scalar(ident[:, :], iota[:, :], pidx[:, 0:1], None, ALU.is_equal).then_inc(s("ident_made"), 1)
            dve.wait_ge(s("src_loaded"), 16 * (EB + 1))
            v.tensor_copy(rowF[:, 1], srcR).then_inc(s("rowF_made"), 1)
            v.tensor_scalar(loI, srcR, P - 1, None, ALU.bitwise_and).then_inc(s("lo_split"), 1)
            ncol = [0]

            def cols_from(dest):
                for h in range(2):
                    n = min(4, EB - 4 * h) * P
                    ncol[0] += 1
                    dve.wait_ge(s("cols_ready"), ncol[0])
                    last = v.tensor_copy(dest[:, 4 * P * h:4 * P * h + n], ps[(ncol[0] - 1) % 2][:, 0:n])
                    last.then_inc(s("cols_copied"), 1)

            cols_from(srcC)
            dve.wait_ge(s("cols_copied"), ncol[0])
            v.tensor_copy(srcC[:, T:T + RT], srcC[:, 0:RT]).then_inc(s("src_cols"), 1)
            dve.wait_ge(s("lo_split"), 1)
            v.tensor_copy(loH[:, :, :], loI).then_inc(s("lo_made"), 1)
            dve.wait_ge(s("lo_made"), 1)
            link(v.tensor_scalar(loI, srcR, 7, None, ALU.arith_shift_right))
            v.tensor_copy(rowF[:, 2], loI).then_inc(s("rowF_made"), 1)
            dve.wait_ge(s("dst_loaded"), 16 * (EB + 1))
            v.tensor_copy(rowF[:, 0], dstR).then_inc(s("rowF_made"), 1)
            dve.wait_ge(s("rowF_made"), 3)
            v.tensor_reduce(dmin[:, :], rowF[:, 0], AX.X, ALU.min).then_inc(s("dmin_made"), 1)
            cols_from(hiC)
            cols_from(rankC)
            dve.wait_ge(s("dmin_turned"), 1)
            link(v.tensor_reduce(base7[:, :], ps[2][0:EB, 0:P].rearrange("a (g t) -> a g t", t=GT), AX.X, ALU.min))
            v.tensor_copy(base7i[:, :], base7[:, :]).then_inc(s("base_made"), 2)
            cols_from(ewC)
            dve.wait_ge(s("cols_copied"), ncol[0])
            split_tmp = t2C[:, :]
            link(v.tensor_copy(ewP[:, :, 0], ewC[:, :]))
            link(v.tensor_tensor(split_tmp, ewC[:, :], ewP[:, :, 0], ALU.subtract))
            link(v.tensor_copy(ewP[:, :, 1], split_tmp))
            link(v.tensor_tensor(split_tmp, split_tmp, ewP[:, :, 1], ALU.subtract))
            v.tensor_copy(ewP[:, :, 2], split_tmp).then_inc(s("ew_split"), 1)
            dve.wait_ge(s("lin_loaded"), 16 * 5)
            v.tensor_tensor(penN[:, :], dL, dnextL, ALU.is_equal)
            link(v.tensor_tensor(sameL[:, :], dL, dprevL, ALU.is_equal))
            link(v.tensor_scalar(penL[:, :], sameL[:, :], -1.0, BIG, ALU.add, ALU.mult))
            link(v.tensor_scalar(penN[:, :], penN[:, :], -1.0, BIG, ALU.add, ALU.mult))
            dve.wait_ge(s("base_loaded"), 32)
            rk = rankC[:, :].rearrange("p (g t) -> p g t", t=GT)
            v.tensor_tensor(rk, rk, baseB[:, :].unsqueeze(2).broadcast_to([P, EB * 16, GT]), ALU.subtract
                            ).then_inc(s("rank_made"), 1)
            dve.wait_ge(s("rank_made"), 1)
            link(v.tensor_scalar(split_tmp, rankC[:, :], float(W), None, ALU.is_ge))
            link(v.scalar_tensor_tensor(split_tmp, rankC[:, :], FAR / 2, split_tmp, ALU.is_lt, ALU.mult))
            v.tensor_reduce(dmin[:, 0:1], split_tmp, AX.X, ALU.max).then_inc(s("wide_found"), 1)
            dve.wait_ge(s("wide_turned"), 1)
            link(v.tensor_reduce(lrow0[:, :], ps[2][0:1, 0:P], AX.X, ALU.max))
            v.tensor_copy(flag[:, :], lrow0[:, :]).then_inc(s("flag_made"), 1)
            dve.wait_ge(s("wprod"), 1)
            v.tensor_copy(fcwT[:, :], ps[3][:, 0:P])
            v.tensor_copy(fcrwT[:, :], ps[3][:, P:2 * P])
            v.tensor_copy(wz[:, :], ps[3][:, 2 * P:3 * P])
            v.tensor_copy(awT[:, :], ps[3][:, 3 * P:3 * P + 3]).then_inc(s("awT_copied"), 1)
            dve.wait_ge(s("awT_copied"), 1)
            v.tensor_copy(a2B[:, :], awT[:, 2:3].broadcast_to([P, P])).then_inc(s("awT_copied"), 1)
            dve.wait_ge(s("wprod"), 2)
            v.tensor_copy(v01[:, :], ps[4][:, 0:2])
            v.tensor_copy(v2B[:, :], ps[4][:, P:2 * P]).then_inc(s("v_made"), 1)
            dve.wait_ge(s("lo_stored"), 16)
            for h in range(2):
                ncol[0] += 1
                n = min(4, EB - 4 * h)
                dve.wait_ge(s("cols_ready"), ncol[0])
                v.tensor_copy(loH[:, 4 * h:4 * h + n, :], ps[(ncol[0] - 1) % 2][:, 0:n * P].rearrange("p (b t) -> p b t", t=P)
                              ).then_inc(s("rank_rows"), 1)

            dve.wait_ge(s("rank_made"), 1)
            dve.wait_ge(s("tails_set"), 5)

            def wide_sums(ph, w, target, psum):
                dst_e, w_e = wide_e[:, 0, :], wide_e[:, 1, :]
                n = ph * G * NB
                if ph == 0:
                    dve.sem_inc(s("wide_added"), 1)
                with dve.Fori(0, G) as g:
                    dve.wait_ge(s("wide_added"), g * NB + (n + 1))
                    v.tensor_scalar(dst_e, rankC[:, ecols(g)], baseB[:, bass.ds(g, 1)], None, ALU.add)
                    v.scalar_tensor_tensor(w_e, rankC[:, ecols(g)], float(W), w[:, ecols(g)], ALU.is_ge, ALU.mult
                                           ).then_inc(s("wide_group"), 1)
                    dve.wait_ge(s("wide_group"), g + (ph * G + 1))
                    dve.sem_inc(s("dve_passed"))
                    with dve.Fori(0, NB) as r:
                        for k in range(GT):
                            last = v.tensor_scalar(S[:, 0, k, :], iota[:, :], dst_e[:, k:k + 1], w_e[:, k:k + 1], ALU.is_equal, ALU.mult)
                        last.then_inc(s("wide_S"), 1)
                        dve.wait_ge(s("wide_summed"), g * NB + r + (n + 1))
                        win = target(r)
                        v.tensor_tensor(win, psum, win, ALU.add)
                        v.tensor_scalar(dst_e, dst_e, float(P), None, ALU.subtract).then_inc(s("wide_added"), 1)
                        dve.wait_ge(s("wide_added"), g * NB + r + (n + 2))

            def deg_onehot(q, slot):
                for k in range(GT - ACT_OH):
                    last = v.tensor_scalar(SH[:, slot, k, 0:W], iota_h[:, :], rankC[:, bass.ds(q * GT + k, 1)], None, ALU.is_equal)
                last.then_inc(s("deg_onehot"), 1)

            deg_onehot(0, 0)
            dve.sem_inc(s("deg_state"), 1)
            with dve.Fori(0, IT) as it:
                first = bases(DVE, it * UG, UG)
                for j in range(UG):
                    deg_onehot(it * UG + (j + 1), (j + 1) % 2)
                    win = deg3[:, bass.ds(first[j], W)]
                    dve.wait_ge(s("deg_state"), it * UG + (j + 1))
                    dve.wait_ge(s("deg_summed"), it * UG + (j + 3))
                    v.tensor_tensor(win, ps[5 + j % 2][0:3, 0:W], win, ALU.add).then_inc(s("deg_state"), 1)
            dve.wait_ge(s("deg_state"), G + 1)
            with any_wide(dve):
                wide_sums(0, ewC, lambda r: deg3[0:1, bass.ds(r * P, P)], ps[2][0:1, 0:W])
            dve.sem_inc(s("deg_made"), 1)
            dve.wait_ge(s("deg_cols"), 1)
            link(v.tensor_scalar(dinv[:, :], ps[7][:, 0:NB], 1.0, None, ALU.add))
            v.tensor_scalar(dtmp[:, 0, :], dinv[:, :], 1e-30, None, ALU.max).then_inc(s("deg_clamped"), 1)
            link(v.tensor_scalar(dtmp[:, 1, :], dinv[:, :], 0.0, None, ALU.is_gt))
            dve.wait_ge(s("deg_root"), 1)
            link(v.reciprocal(dtmp[:, 0, :], dtmp[:, 0, :]))
            link(v.tensor_tensor(dinv[:, :], dtmp[:, 0, :], dtmp[:, 1, :], ALU.mult))
            dve.wait_ge(s("x_loaded"), 16 * 7)
            dve.sem_inc(s("x1_evac"), 2)
            with dve.Fori(0, NCH) as c:
                for b in range(NC):
                    last = v.tensor_scalar(rows[:, c * NC + b, :], xsb[:, c * NC + b, :],
                                           dinv[:, bass.ds(c * NC + b, 1)], None, ALU.mult)
                last.then_inc(s("x1_made"), 1)

            def split3(parts, full, tmp):
                link(v.tensor_copy(parts[:, 0, :], full))
                link(v.tensor_tensor(tmp, full, parts[:, 0, :], ALU.subtract))
                link(v.tensor_copy(parts[:, 1, :], tmp))
                link(v.tensor_tensor(tmp, tmp, parts[:, 1, :], ALU.subtract))
                v.tensor_copy(parts[:, 2, :], tmp).then_inc(s("tables_split"), 1)

            def onehots(r, q, i, j):
                dve.wait_ge(lo_loaded[j], i * 16 + 16 * (r * (G // 2 + 1) + 1))
                last = v.tensor_scalar(ohL[:, j, :], loB[:, j, :], pidx[:, 0:1], None, ALU.is_equal)
                if r:
                    dve.wait_ge(rank_loaded[j], i * 16 + 16)
                    last = v.tensor_scalar(ohR[:, j, :], rankB[:, j, :], pidx[:, 0:1], None, ALU.is_equal)
                last.then_inc(s("onehot_built"), 1)

            def lookups(r, dest):
                onehots(r, 0, 0, 0)
                with dve.Fori(0, G // 2) as i:
                    for j in range(2):
                        q = i * 2 + j
                        onehots(r, q + 1, i + j, (j + 1) % 2)
                        dve.wait_ge(s("looked_up"), i * 2 + (j + 1 + r * G))
                        if r:
                            v.tensor_tensor(eC[:, ecols(q)], ps[2 + j][:, 0:GT], t2C[:, ecols(q)], ALU.add)
                        dve.wait_ge(s("selected"), i * 2 + (j + 1 + r * G))
                        for k in range(GT):
                            col = bass.ds(q * GT + k, 1)
                            last = v.scalar_tensor_tensor(prod[:, k, :], iota[:, 0:NB], hiC[:, col], ps[4 + j][:, 64 * k:64 * k + NB],
                                                          ALU.is_equal, ALU.mult, accum_out=dest[:, col])
                        last.then_inc(s("selected"), 1)

            dve.wait_ge(s("x1_evac"), 2 * NCH + 2)
            split3(tab, dinv[:, :], dtmp[:, 1, :])
            dve.sem_inc(s("selected"), 1)
            lookups(0, t2C)
            dve.wait_ge(s("selected"), G + 1)
            link(v.tensor_tensor(t2C[:, 0:T], t2C[:, 0:T], ewC[:, 0:T], ALU.mult))
            def build_S(q, slot, wcols, pair=None):
                for k in range(GT):
                    col = bass.ds(q * GT + k, 1)
                    last = v.tensor_scalar(S[:, slot, k, :], iota[:, :], rankC[:, col], wcols[:, col], ALU.is_equal, ALU.mult)
                    if pair and k % 2:
                        piece(*pair, k // 2)
                last.then_inc(s("S_built"), 1)

            def edge_pass(p, wcols):
                naccs = 2 if p == 2 else 1
                build_S(0, 0, wcols)
                with dve.Fori(0, IT) as it:
                    if p == 1:
                        first = bases(DVE, it * UG, UG)
                    else:
                        halves = bases(DVE, it * RG, RG), bases(DVE, it * RG + HG, RG)
                        first = [halves[j % 2][j // 2] for j in range(UG)]
                    for j in range(UG):
                        q, _ = group(p, it, j)
                        if p == 1:
                            pass1_step(q, it, j)
                        else:
                            build_S(group(p, it, j + 1)[0], (j + 1) % 2, wcols)
                        win = acc[:, 0:naccs, bass.ds(first[j], W)]
                        dve.wait_ge(s("acc_added"), it * UG + (p * (G + 1) + j + 1))
                        dve.wait_ge(s("summed"), it * UG + summed_by(p, j + 1))
                        v.tensor_tensor(win, ps[2 + j % 2][:, 0:naccs * W].rearrange("p (a w) -> p a w", a=naccs), win, ALU.add
                                        ).then_inc(s("acc_added"), 1)

            dve.sem_inc(s("acc_added"), 1)
            edge_pass(0, t2C)
            dve.wait_ge(s("acc_added"), G + 1)
            with any_wide(dve):
                wide_sums(1, t2C, lambda r: acc[:, 0:1, bass.ds(r * P, P)],
                          ps[2][:, 0:W].rearrange("p (a w) -> p a w", w=W))
            dve.sem_inc(s("sums_made"), 1)
            dve.sem_inc(s("l1_free"), 3)
            dve.sem_inc(s("h1_evac"), 2)
            for b in range(NB):
                dve.wait_ge(s("l1_prod"), b + 1)
                if b >= NC:
                    dve.wait_ge(s("h1_made"), b - NC + 1)
                v.scalar_tensor_tensor(u[:, b % NC, :], ps[4 + b % NC % 4][:, 0:D], dinv[:, b:b + 1], b1B[:, :], ALU.mult, ALU.add
                                       ).then_inc(s("l1_free"), 1)

            def away_from(it, m):
                uses = IDS.count(IDS[m]) if m >= 0 else 0
                first = 1 if IDS[m] == IDS[-1] else 0
                dve.wait_ge(ids_loaded[IDS[m]], it * (16 * uses) + 16 * (first + IDS[:m + 1].count(IDS[m])))
                dve.wait_ge(s("oh_built"), it * (RG * DP) + ((m + 1) * DP + 1))
                dve.wait_ge(s("oh_built_act"), it * (RG * AP) + (m + 2) * AP)
                dve.sem_inc(s("dve_passed"))
                v.tensor_scalar(away, ids[:, IDS[m], :], pidx[:, 0:1], None, ALU.subtract).then_inc(s("ids_used"), 1)
                dve.wait_ge(s("ids_used"), it * RG + (m + 4))

            def piece(it, m, c):
                dve.wait_ge(s("oh_used"), it * (RG * NP) + (NP + (m + 1) * NP + (c - 1 if c > 1 else last_like(c, DP) + 1 - NP)))
                v.tensor_tensor(ohV[:, c % 2, :, :], away.unsqueeze(1).broadcast_to([P, CB, P]),
                                blk0[:, c * CB:(c + 1) * CB].unsqueeze(2).broadcast_to([P, CB, P]), ALU.is_equal
                                ).then_inc(s("oh_built"), 1)

            def pass1_step(q, it, j):
                if j % 2 == 0:
                    away_from(it, j // 2)
                    build_S(q + 1, (j + 1) % 2, ewC, (it, j // 2))
                else:
                    build_S(q + 1, (j + 1) % 2, ewC)
                dve.wait_ge(rh_loaded[j % 2], it * (16 * UG // 2) + (16 * (j // 2 + 1)))
                dve.sem_inc(s("dve_passed"))
                for k in range(GT):
                    last = v.scalar_tensor_tensor(rh[:, j % 2, k, :], rh[:, j % 2, k, :], 1.0, v2B[:, :], ALU.mult, ALU.mult,
                                                  accum_out=t2C[:, bass.ds(q * GT + k, 1)])
                    if j % 2 == 0 and k % 2 and GT // 2 + k // 2 < DP:
                        piece(it, j // 2, GT // 2 + k // 2)
                last.then_inc(s("rh_dotted"), 1)

            dve.sem_inc(s("ids_used"), 2)
            dve.sem_inc(s("rh_dotted"), 2)
            dve.sem_inc(s("oh_built"), 1)
            v.tensor_scalar(nblk0, iota[:, 0:NB], -float(P), None, ALU.mult)
            v.tensor_scalar(blk0, iota[:, 0:NB], float(P), None, ALU.mult).then_inc(s("blk0_made"), 1)
            dve.wait_ge(s("blk0_made"), 1)
            dve.wait_ge(s("h1_evac"), 2 * NCH + 2)
            dve.sem_inc(s("acc_added"), 1)
            away_from(0, -1)
            for c in range(DP):
                piece(0, -1, c)
            edge_pass(1, ewC)

            dve.wait_ge(s("acc_added"), 2 * G + 2)
            with any_wide(dve):
                wide_sums(2, ewC, lambda r: acc[:, 0:1, bass.ds(r * P, P)],
                          ps[2][:, 0:W].rearrange("p (a w) -> p a w", w=W))
            dve.sem_inc(s("sums_made"), 1)
            dve.sem_inc(s("l2_free"), 3)
            dve.sem_inc(s("x2_evac"), 2)
            dve.wait_ge(s("h1_stored"), 16 * NCH)
            LAG = 3
            for b in range(NB + LAG):
                if b < NB:
                    dve.wait_ge(s("l2_prod"), b + 1)
                    v.scalar_tensor_tensor(pre1[:, b, :], ps[4 + b % NC % 4][:, 0:D], dinv[:, b:b + 1], b2B[:, :], ALU.mult, ALU.add
                                           ).then_inc(s("l2_free"), 1)
                if b >= LAG:
                    dve.wait_ge(s("l2_res"), b - LAG + 1)
                    v.bn_stats(bst[:, b - LAG, :], pre1[:, b - LAG, :]).then_inc(s("bn_done"), 1)
            dve.wait_ge(s("bn_done"), NB)
            for b in range(NB):
                last = v.bn_aggr(mv[:, b, :], bst[:, b, :])
            last.then_inc(s("stats_made"), 1)
            dve.wait_ge(s("std_made"), 1)
            link(v.reciprocal(rs[:, :], sd[:, :]))
            v.scalar_tensor_tensor(nmr[:, :], mv[:, :, 0], -1.0, rs[:, :], ALU.mult, ALU.mult).then_inc(s("scale_made"), 1)
            for c in range(NCH):
                for b in range(c * NC, c * NC + NV):
                    last = v.tensor_scalar(xsb[:, b, :], pre1[:, b, :], mv[:, b, 0:1], rs[:, b:b + 1], ALU.subtract, ALU.mult)
                last.then_inc(s("x2_made"), 1)
            dve.wait_ge(s("x2_made"), NCH)
            dve.wait_ge(s("x2_made_act"), NCH)
            v.memset(s1P, 0.0).then_inc(s("s1_cleared"), 1)

            dve.wait_ge(s("scores"), 1)
            score = ps[6][:, 0:2 * NB].rearrange("p (b k) -> p b k", k=2)
            v.tensor_copy(tabf[:, :], score[:, :, 0])
            link(v.tensor_copy(s1f[:, 0:NB], score[:, :, 1]))
            split3(s1p, s1f[:, 0:NB], dtmp[:, 0, :])
            split3(tab, tabf[:, :], dtmp[:, 1, :])
            dve.wait_ge(s("s1_turned"), 1)
            v.tensor_copy(s1rows[:, :, :], ps[1][0:NB, 0:3 * 64].bitcast(BF16).rearrange("a (k p) -> a k p", k=3)
                          ).then_inc(s("s1_rows"), 1)
            dve.wait_ge(s("windows"), IT)
            link(v.tensor_copy(s1f[:, :], ps[7][:, 0:G]))
            split3(s1w, s1f[:, :], selC[:, 0:G])

            lookups(1, selC)
            dve.wait_ge(s("selected"), 2 * G + 1)
            with any_wide(dve):
                dst_e, got, here = (wide_e[:, k, :] for k in range(3))
                v.memset(iow[:, :], 0.0)
                v.tensor_copy(S[:, 1, 0, :], v01[:, 1:2].broadcast_to([P, P])).then_inc(s("wide_s1_used"), 1)
                dve.sem_inc(s("wide_s1_added"), 1)
                dve.wait_ge(s("wide_s1_used"), 1)
                with dve.Fori(0, NB) as r:
                    dve.wait_ge(s("wide_s1"), r + 1)
                    dve.sem_inc(s("dve_passed"))
                    with dve.Fori(0, G) as g:
                        dve.wait_ge(s("wide_s1_added"), r * G + g + 1)
                        v.tensor_scalar(dst_e, rankC[:, ecols(g)], baseB[:, bass.ds(g, 1)], None, ALU.add
                                        ).then_inc(s("wide_s1_step"), 1)
                        dve.wait_ge(s("wide_s1_step"), r * (4 * G) + g * 4 + 1)
                        v.tensor_scalar(dst_e, dst_e, iow[:, 0:1], None, ALU.subtract).then_inc(s("wide_s1_step"), 1)
                        dve.wait_ge(s("wide_s1_step"), r * (4 * G) + g * 4 + 2)
                        for k in range(GT):
                            last = v.scalar_tensor_tensor(S[:, 0, k, :], iota[:, :], dst_e[:, k:k + 1], ps[2][:, 0:P],
                                                          ALU.is_equal, ALU.mult, accum_out=got[:, k:k + 1])
                        last.then_inc(s("wide_s1_step"), 1)
                        dve.wait_ge(s("wide_s1_step"), r * (4 * G) + g * 4 + 3)
                        v.scalar_tensor_tensor(here, rankC[:, ecols(g)], float(W), got, ALU.is_ge, ALU.mult
                                               ).then_inc(s("wide_s1_step"), 1)
                        dve.wait_ge(s("wide_s1_step"), r * (4 * G) + g * 4 + 4)
                        v.tensor_tensor(eC[:, ecols(g)], eC[:, ecols(g)], here, ALU.add).then_inc(s("wide_s1_added"), 1)
                    v.tensor_scalar(iow[:, :], iow[:, :], float(P), None, ALU.add).then_inc(s("wide_s1_used"), 1)
                    dve.wait_ge(s("wide_s1_used"), r + 2)
                dve.wait_ge(s("wide_s1_added"), NB * G + 1)
            v.memset(eC[:, T:TP], 0.0)
            link(v.tensor_tensor(eC[:, 0:T], eC[:, 0:T], selC[:, 0:T], ALU.add))
            v.scalar_tensor_tensor(eC[:, 0:T], eC[:, 0:T], SLOPE, eC[:, 0:T], ALU.mult, ALU.max).then_inc(s("e_cols"), 1)
            for h in range(2):
                n = min(4, EB - 4 * h)
                dve.wait_ge(s("e_turned"), h + 1)
                v.tensor_copy(rowF[:, 0, 4 * h:4 * h + n, :], ps[h][:, 0:n * P].rearrange("p (b t) -> p b t", t=P)).then_inc(s("e_rows"), 1)

            nscan = [0]

            def run_scan(out_, data, pen, op0, op1, neutral, reverse):
                n = nscan[0]
                nscan[0] += 1
                d, p_, o = (a[:, ::-1] if reverse else a for a in (data, pen, out_))
                v.tensor_tensor_scan(o, p_, d, neutral, op0, op1).then_inc(s("dve_step"), 1)
                steps[0] += 1
                link(v.tensor_reduce(lend[0:LP, 1:2], pen, AX.X, ALU.min))
                end = 0 if reverse else LW - 1
                v.tensor_copy(lend[0:LP, 0:1], out_[:, end:end + 1]).then_inc(s("ends_made"), 1)
                dve.wait_ge(s("ends_turned"), n + 1)
                link(v.tensor_copy(lrow[:, :, 0:LP], ps[6][0:1, 0:2 * P].rearrange("a (k p) -> a k p", k=2)[:, :, 0:LP]))
                link(v.memset(lcar[:, :], neutral))
                r0, r1, rc = lrow[0:1, 0, 0:LP], lrow[0:1, 1, 0:LP], lcar[0:1, 1:LP + 1]
                if reverse:
                    r0, r1, rc = r0[:, ::-1], r1[:, ::-1], rc[:, ::-1]
                v.tensor_tensor_scan(rc, r1, r0, neutral, op0, op1).then_inc(s("carry_made"), 1)
                dve.wait_ge(s("carry_turned"), n + 1)
                link(v.tensor_copy(lini[0:LP, :], ps[7][0:LP, 0:1]))
                link(v.tensor_tensor_scan(o, p_, d, lini[0:LP, 0:1], op0, op1))

            dve.wait_ge(s("e_loaded"), 16)
            run_scan(mL, eL, penL[:, :], ALU.add, ALU.max, -BIG, False)
            run_scan(tL, mL, penN[:, :], ALU.add, ALU.max, -BIG, True)
            v.tensor_tensor(eL, eL, tL, ALU.subtract).then_inc(s("e_shifted"), 1)
            dve.wait_ge(s("e_exp"), 1)
            run_scan(mL, eL, sameL[:, :], ALU.mult, ALU.add, 0.0, False)
            run_scan(tL, mL, penN[:, :], ALU.add, ALU.max, -BIG, True)
            link(v.reciprocal(tL, tL))
            link(v.memset(rowF[:, 0, EB - 1, :], 0.0))
            v.tensor_tensor(mL, eL, tL, ALU.mult).then_inc(s("alpha_made"), 1)
            for h in range(2):
                n = min(4, EB - 4 * h) * P
                dve.wait_ge(s("alpha_turned"), h + 1)
                link(v.tensor_copy(eC[:, 4 * P * h:4 * P * h + n], ps[h][:, 0:n]))
            v.memset(acc[:, :, :], 0.0).then_inc(s("acc_added"), 1)
            edge_pass(2, eC)

            dve.wait_ge(s("acc_added"), 3 * G + 3)
            with any_wide(dve):
                wide_sums(3, eC, lambda r: acc[:, 0:2, bass.ds(r * P, P)],
                          ps[2][:, 0:2 * W].rearrange("p (a w) -> p a w", w=W))
            dve.sem_inc(s("sums_made"), 1)
            dve.sem_inc(s("out_made"), 1)

            def out_sum(b):
                dve.wait_ge(s("fin_prod"), b + 1)
                v.scalar_tensor_tensor(pre2[:, b, :], out_bank(b % FB), 0.0, xsb[:, b, :], ALU.max, ALU.add).then_inc(s("fin_free"), 1)

            def out_scale(c):
                blks = slice(c * NC, (c + 1) * NC)
                dve.wait_ge(s("std_made"), c + 2)
                link(v.reciprocal(rs[:, blks], sd[:, blks]))
                v.scalar_tensor_tensor(nmr[:, blks], mv[:, blks, 0], -1.0, rs[:, blks], ALU.mult, ALU.mult).then_inc(s("scale_made"), 1)

            LAG = 2
            for b in range(NB + LAG):
                if b < NB:
                    out_sum(b)
                a = b - LAG
                if a >= 0:
                    dve.wait_ge(s("fin_free"), a + 1)
                    v.bn_stats(bst[:, a, :], pre2[:, a, :]).then_inc(s("bn_done"), 1)
                    if a % NC == NC - 1:
                        dve.wait_ge(s("bn_done"), NB + a + 1)
                        for k in range(a - NC + 1, a + 1):
                            last = v.bn_aggr(mv[:, k, :], bst[:, k, :])
                        last.then_inc(s("stats_made"), 1)
                    if a % NC == NC // 2 and a > NC:
                        out_scale(a // NC - 1)
            out_scale(NCH - 1)



_INS = ['x', 'src', 'dst', 'edge_attr_128', 'edge_weight', 'L0_gnn_W1', 'L0_gnn_b1', 'L0_gnn_W2', 'L0_gnn_b2', 'L1_gnn_fc_w', 'L1_gnn_fc_r_w', 'L1_gnn_attn_w', 'L1_gnn_loop_w']
_OUTS = [((6250, 128), 'float32')]


def kernel(**inputs):
    import numpy as _np
    import concourse.bacc as _bacc
    from concourse import mybir as _mybir
    from concourse.bass_utils import run_bass_kernel_spmd as _run

    nc = _bacc.Bacc("TRN2", target_bir_lowering=False, num_devices=1)
    arrays, args = {}, []
    for name in _INS:
        a = _np.ascontiguousarray(inputs[name])
        arrays[f"in_{name}_dram"] = a
        args.append(nc.dram_tensor(f"in_{name}_dram", a.shape, _mybir.dt.from_np(a.dtype), kind="ExternalInput").ap())
    for i, (shape, dtype) in enumerate(_OUTS):
        dt = _mybir.dt.from_np(_np.dtype(dtype))
        args.append(nc.dram_tensor(f"out_{i}_dram", shape, dt, kind="ExternalOutput").ap())
    build(nc, *args)
    r = _run(nc, [arrays], core_ids=[0])
    got = tuple(r.results[0][f"out_{i}_dram"] for i in range(len(_OUTS)))
    return got[0]
```
